# Optimizing a Trainium2 kernel written in Bass

```python
import numpy as np
import jax
import jax.numpy as jnp

def _softmax(x, axis=-1):
    return jax.nn.softmax(x, axis=axis)

def _gelu(x):
    return jax.nn.gelu(x, approximate=True)

def _silu(x):
    return jax.nn.silu(x)

def _sigmoid(x):
    return jax.nn.sigmoid(x)

def _layernorm(x, axis=-1, eps=1e-05):
    m = jnp.mean(x, axis=axis, keepdims=True)
    v = jnp.var(x, axis=axis, keepdims=True)
    return (x - m) / jnp.sqrt(v + eps)

def _scatter_add(tgt, idx, src, axis=0):
    return tgt.at[idx].add(src)

def _segment_sum(src, seg, n):
    return jax.ops.segment_sum(src, seg, n)
kernel_name = 'mk_xattn_ffn_d1_seqx_r8_871bef'

def setup_inputs(seed: int=0):
    np.random.seed(seed)
    _w = jnp.asarray

    def _rec_inputs():
        import jax
        import jax.numpy as jnp
        _rk = jax.random.key(seed)
        x = -0.0002928 + 1 * jax.random.normal(jax.random.fold_in(_rk, 1), (1, 1024, 128), jnp.float32)
        _lenS = 1024 - jax.random.randint(jax.random.fold_in(_rk, 7), (1,), 0, max(1, 1024 // 4) + 1, jnp.int32)
        _lenS2 = 6404 - jax.random.randint(jax.random.fold_in(_rk, 8), (1,), 0, max(1, 6404 // 4) + 1, jnp.int32)
        _ctx_768P = jax.random.normal(jax.random.fold_in(_rk, 11), (1, 16, 96), jnp.float32)
        _ctx_768c = jax.random.dirichlet(jax.random.fold_in(_rk, 511), 0.3 * jnp.ones((16,), jnp.float32), (1, 6404))
        _ctx_768t = jnp.einsum('bsk,bkd->bsd', _ctx_768c, _ctx_768P)
        _ctx_768t = _ctx_768t * jax.lax.rsqrt(jnp.mean(jnp.square(_ctx_768t)) + 1e-12) * 0.953939
        ctx_768 = 2.09791e-05 + 1.00001 * (_ctx_768t + 0.3 * jax.random.normal(jax.random.fold_in(_rk, 611), (1, 6404, 96), jnp.float32))
        return (x, ctx_768)
    x, ctx_768 = _rec_inputs()

    def _L0_xattn_setup():
        import jax, jax.numpy as jnp
        import numpy as np
        H = 8
        D = 64
        SCALE = D ** (-0.5)
        key = jax.random.key(seed)
        ks = jax.random.split(key, 7)
        B, Nq, Nkv = (2, 256, 256)
        Cq, Ck, I = (128, 96, H * D)
        return {'x': jax.random.normal(ks[0], (B, Nq, Cq), jnp.float32), 'context': jax.random.normal(ks[1], (B, Nkv, Ck), jnp.float32), 'Wq': jax.random.normal(ks[2], (Cq, I), jnp.float32) * Cq ** (-0.5), 'Wk': jax.random.normal(ks[3], (Ck, I), jnp.float32) * Ck ** (-0.5), 'Wv': jax.random.normal(ks[4], (Ck, I), jnp.float32) * Ck ** (-0.5), 'Wo': jax.random.normal(ks[5], (I, Cq), jnp.float32) * I ** (-0.5), 'bo': jnp.zeros((Cq,), jnp.float32)}
    _L0_xattn_all = _L0_xattn_setup()
    _L0_xattn_in = {k: v for k, v in _L0_xattn_all.items() if k in ('Wq', 'Wk', 'Wv', 'Wo', 'bo')}
    del _L0_xattn_all

    def _L0_ffn_setup():
        import jax, jax.numpy as jnp
        import numpy as np
        from jax import lax
        T, B, I, M, O = (32, 64, 128, 128, 128)

        def _xavier(key, shape):
            fan_out, fan_in = shape
            limit = float(np.sqrt(6.0 / (fan_in + fan_out)))
            return jax.random.uniform(key, shape, jnp.float32, -limit, limit)
        key = jax.random.key(seed)
        ks = jax.random.split(key, 9)
        x = jax.random.normal(ks[0], (T, B, I), jnp.float32)
        return {'x': x, 'wf': _xavier(ks[1], (M, I)), 'uf': _xavier(ks[2], (M, M)), 'bf': jnp.zeros((M,), jnp.float32), 'wi': _xavier(ks[3], (M, I)), 'ui': _xavier(ks[4], (M, M)), 'bi': jnp.zeros((M,), jnp.float32), 'wc': _xavier(ks[5], (M, I)), 'uc': _xavier(ks[6], (M, M)), 'bc': jnp.zeros((M,), jnp.float32), 'wo': _xavier(ks[7], (O, I)), 'uo': _xavier(ks[8], (O, M)), 'bo': jnp.zeros((O,), jnp.float32), 'in_c': jnp.zeros((M,), jnp.float32)}
    _L0_ffn_all = _L0_ffn_setup()
    _L0_ffn_in = {k: v for k, v in _L0_ffn_all.items() if k in ('wf', 'uf', 'bf', 'wi', 'ui', 'bi', 'wc', 'uc', 'bc', 'wo', 'uo', 'bo', 'in_c')}
    del _L0_ffn_all
    return {'x': x, 'ctx_768': ctx_768, 'L0_xattn_Wq': _L0_xattn_in['Wq'], 'L0_xattn_Wk': _L0_xattn_in['Wk'], 'L0_xattn_Wv': _L0_xattn_in['Wv'], 'L0_xattn_Wo': _L0_xattn_in['Wo'], 'L0_xattn_bo': _L0_xattn_in['bo'], 'L0_ffn_wf': _L0_ffn_in['wf'], 'L0_ffn_uf': _L0_ffn_in['uf'], 'L0_ffn_bf': _L0_ffn_in['bf'], 'L0_ffn_wi': _L0_ffn_in['wi'], 'L0_ffn_ui': _L0_ffn_in['ui'], 'L0_ffn_bi': _L0_ffn_in['bi'], 'L0_ffn_wc': _L0_ffn_in['wc'], 'L0_ffn_uc': _L0_ffn_in['uc'], 'L0_ffn_bc': _L0_ffn_in['bc'], 'L0_ffn_wo': _L0_ffn_in['wo'], 'L0_ffn_uo': _L0_ffn_in['uo'], 'L0_ffn_bo': _L0_ffn_in['bo'], 'L0_ffn_in_c': _L0_ffn_in['in_c']}

def reference(x, ctx_768, L0_xattn_Wq, L0_xattn_Wk, L0_xattn_Wv, L0_xattn_Wo, L0_xattn_bo, L0_ffn_wf, L0_ffn_uf, L0_ffn_bf, L0_ffn_wi, L0_ffn_ui, L0_ffn_bi, L0_ffn_wc, L0_ffn_uc, L0_ffn_bc, L0_ffn_wo, L0_ffn_uo, L0_ffn_bo, L0_ffn_in_c):
    import jax
    import jax.numpy as jnp

    def _L0_xattn_ref(x, context, Wq, Wk, Wv, Wo, bo):
        import jax, jax.numpy as jnp
        import numpy as np
        H = 8
        D = 64
        SCALE = D ** (-0.5)
        B, Nq, _ = x.shape
        Nkv = context.shape[1]
        q = (x @ Wq).reshape(B, Nq, H, D)
        k = (context @ Wk).reshape(B, Nkv, H, D)
        v = (context @ Wv).reshape(B, Nkv, H, D)
        sim = jnp.einsum('bihd,bjhd->bhij', q, k) * SCALE
        attn = jax.nn.softmax(sim, axis=-1)
        out = jnp.einsum('bhij,bjhd->bihd', attn, v).reshape(B, Nq, H * D)
        return out @ Wo + bo

    def _L0_ffn_ref(x, wf, uf, bf, wi, ui, bi, wc, uc, bc, wo, uo, bo, in_c):
        import jax, jax.numpy as jnp
        import numpy as np
        from jax import lax
        T, B, I, M, O = (32, 64, 128, 128, 128)

        def _xavier(key, shape):
            fan_out, fan_in = shape
            limit = float(np.sqrt(6.0 / (fan_in + fan_out)))
            return jax.random.uniform(key, shape, jnp.float32, -limit, limit)
        batch = x.shape[1]
        c0 = jnp.broadcast_to(in_c, (batch, in_c.shape[0]))

        def step(c, xt):
            ft = jax.nn.sigmoid(xt @ wf.T + c @ uf.T + bf)
            it = jax.nn.sigmoid(xt @ wi.T + c @ ui.T + bi)
            gt = jnp.tanh(xt @ wc.T + c @ uc.T + bc)
            c = ft * c + it * gt
            return (c, None)
        c_final, _ = lax.scan(step, c0, x)
        h = jnp.tanh(jnp.einsum('tbi,oi->tbo', x, wo) + c_final @ uo.T + bo)
        return h
    x = x + _L0_xattn_ref(_layernorm(x, axis=-1), ctx_768, L0_xattn_Wq, L0_xattn_Wk, L0_xattn_Wv, L0_xattn_Wo, L0_xattn_bo)
    x = x + _L0_ffn_ref(_layernorm(x, axis=-1), L0_ffn_wf, L0_ffn_uf, L0_ffn_bf, L0_ffn_wi, L0_ffn_ui, L0_ffn_bi, L0_ffn_wc, L0_ffn_uc, L0_ffn_bc, L0_ffn_wo, L0_ffn_uo, L0_ffn_bo, L0_ffn_in_c)
    return x

_drawn_inputs = setup_inputs


def setup_inputs(seed=0):
    import zlib

    import numpy as np

    out = dict(_drawn_inputs(seed))
    spreads = {'L0_xattn_bo': (0.0, 0.1),
     'L0_ffn_bf': (0.0, 2.0),
     'L0_ffn_bi': (0.0, 0.8),
     'L0_ffn_bc': (0.0, 0.524),
     'L0_ffn_bo': (0.0, 0.1),
     'L0_ffn_in_c': (0.0, 0.278)}
    factors = {'L0_ffn_wf': 6.303, 'L0_ffn_uf': 22.306, 'L0_ffn_ui': 8.0, 'L0_ffn_uc': 3.558}
    for name, (base, spread) in spreads.items():
        noise = np.random.default_rng([zlib.crc32(name.encode()), seed]).standard_normal(out[name].shape)
        drawn = base * np.exp(spread * noise) if base else spread * noise
        out[name] = jnp.asarray(drawn.astype(out[name].dtype))
    for name, factor in factors.items():
        out[name] = (out[name] * factor).astype(out[name].dtype)
    return out
```

```python
from contextlib import ExitStack

import numpy as np

import concourse.bass as bass
from concourse import mybir

F32 = mybir.dt.float32
BF16 = mybir.dt.bfloat16
ALU = mybir.AluOpType
ACT = mybir.ActivationFunctionType
AX = mybir.AxisListType
ds = bass.ds

P = 128
HEADS = 8
DH = 64
DM = 128
DC = 96
NQ = 1024
NKV = 6404
SCALE = DH ** -0.5
EPS = 1e-5

TILES = (NKV + P - 1) // P
WHOLE = NKV // P
LAST = NKV - WHOLE * P
UNROLL = 3
TURNS = TILES // UNROLL
CHUNK = UNROLL * P
QG = 512
QT = QG // P
HALVES = NQ // QG
VW = 2 * DH + 1
AUG = DC + 2
POOL_COLS = 320
MX = TURNS * QT
KEYS = TILES * P
LN_STEPS = 8

assert TILES % UNROLL == 0 and HEADS % 2 == 0 and 2 * HALVES * QG == 2 * NQ

def bank_uses(first, last, half):
    uses = [("minus_max", half)]
    if half == 0:
        uses += [] if last else [("K", 0)]
        uses += [] if first else [("Y", 0)]
        uses += [] if last else [("QP", 0), ("QL", 0)] + [("K", i) for i in range(1, TURNS)]
        uses += [] if first else [("OT", 0)]
    else:
        uses += [] if first else [("Y", 1)]
        uses += [] if last else [("QP", 1), ("QL", 1)]
        uses += [("OT", 1)]
    return uses


def head_uses(first, last):
    return bank_uses(first, last, 0) + bank_uses(first, last, 1)


PRO_USES = [("QP", 0), ("QL", 0), ("QP", 1), ("QL", 1)] + [("K", i) for i in range(TURNS)]
TAIL_USES = [("Y", 0), ("OT", 0), ("Y", 1)]
BASE_0 = len(PRO_USES)
BASE_1 = BASE_0 + len(head_uses(True, False))
PER_HEAD = len(head_uses(False, False))
BASE_LAST = BASE_1 + (HEADS - 2) * PER_HEAD
BASE_TAIL = BASE_LAST + len(head_uses(False, True))


def build(nc, x, ctx_768, Wq, Wk, Wv, Wo, xbo, wf, uf, bf, wi, ui, bi, wc, uc, bc, wo, uo, fbo, in_c, out):
    stack = ExitStack()
    with stack:
        def sb(name, shape, dt):
            return stack.enter_context(nc.sbuf_tensor(name, shape, dt))

        def sem(name):
            return stack.enter_context(nc.semaphore(name))

        V = sb("V", [P, TILES * HEADS * VW], BF16)
        V4 = V[:, :].rearrange("p (t h c) -> p t h c", t=TILES, h=HEADS)
        K = sb("K", [P, 2 * KEYS], BF16)
        ctx_hi = sb("ctx_hi", [P, KEYS], BF16)
        ctx_lo = sb("ctx_lo", [P, KEYS], BF16)
        prob = sb("prob", [P, UNROLL, QG], F32)
        prob_lo = sb("prob_lo", [P, UNROLL, QG], BF16)
        qA = sb("qA", [P, 2, NQ], BF16)
        qB = sb("qB", [P, 2, NQ], BF16)
        q_low = sb("q_low", [P, QG], BF16)
        xnT_hi = sb("xnT_hi", [P, NQ], BF16)
        xnT_lo = sb("xnT_lo", [P, NQ], BF16)
        WqD_hi = sb("WqD_hi", [P, HEADS, 2, DH], BF16)
        WqD_lo = sb("WqD_lo", [P, HEADS, 2, DH], BF16)
        WkD_hi = sb("WkD_hi", [DC, HEADS, 2, DH], BF16)
        WkD_lo = sb("WkD_lo", [DC, HEADS, 2, DH], BF16)
        Wv_hi = sb("Wv_hi", [DC, HEADS * DH], BF16)
        Wv_lo = sb("Wv_lo", [DC, HEADS * DH], BF16)
        WkT = sb("WkT", [P, HEADS * DC], BF16)
        Wo_hi = sb("Wo_hi", [P, HEADS * DM], BF16)
        Wo_lo = sb("Wo_lo", [P, HEADS * DM], BF16)
        gateT = sb("gateT", [P, 5, P], F32)
        acc_raw = sb("acc_raw", [P, QT, VW], F32)
        o_norm = sb("o_norm", [P, QT, DH], F32)
        oT = sb("oT", [P, QG], BF16)
        yT = sb("yT", [P, NQ], F32)
        part_max = sb("part_max", [P, QT, TURNS], F32)
        neg_max = sb("neg_max", [P, QT], F32)
        neg_max2 = sb("neg_max2", [P, QT, 2], BF16)
        rden = sb("rden", [P, QT], F32)
        ident = sb("ident", [P, P], F32)
        identb = sb("identb", [P, P], BF16)
        stat = sb("stat", [P, 4, 8], F32)
        cols = sb("cols", [P, 8], F32)
        gate_bias = sb("gate_bias", [P, 3], F32)

        oT4 = oT[:, :].rearrange("p (k a q) -> p k a q", k=QT // 2, a=2)

        raw = V[:, :].bitcast(F32)
        ctx_raw = raw[:, 0:TILES * DC].rearrange("p (t c) -> p t c", t=TILES)
        at = 16000
        x_raw = raw[:, at:at + NQ].rearrange("p (n d) -> p n d", d=DM)
        x_sq = raw[:, at + 8 * NQ - 2048:at + 9 * NQ - 2048].rearrange("p (n d) -> p n d", d=DM)
        Wq_raw = raw[:, at + 1024:at + 1536]
        Wk_raw = raw[0:DC, at + 1536:at + 2048]
        Wv_raw = raw[0:DC, at + 2048:at + 2560]
        Wo_raw = raw[:, at + 2560:at + 3584]
        gate_raw = raw[:, at + 3584:at + 3584 + 8 * P].rearrange("p (w c) -> p w c", w=8)
        cbc = raw[:, at + 4608:at + 4608 + P]
        gsum = raw[:, at + 4736:at + 4736 + 3 * P].rearrange("p (w c) -> p w c", w=3)
        late = ctx_lo[:, :].bitcast(F32)
        x_late = late[:, 0:NQ].rearrange("p (n d) -> p n d", d=DM)
        x1 = late[:, NQ:2 * NQ].rearrange("p (n d) -> p n d", d=DM)
        xc = late[:, 2 * NQ:3 * NQ].rearrange("p (n d) -> p n d", d=DM)
        after = V[:, :].bitcast(F32)
        sq2 = after[:, 0:NQ].rearrange("p (n d) -> p n d", d=DM)
        xn2T = after[:, NQ:2 * NQ]
        fT = after[:, 2 * NQ:3 * NQ]
        iT = after[:, 3 * NQ:4 * NQ]
        gT = after[:, 4 * NQ:5 * NQ]
        cT = after[:, 5 * NQ:6 * NQ]
        hT = after[:, 6 * NQ:7 * NQ]
        res = after[:, 7 * NQ:8 * NQ].rearrange("p (n d) -> p n d", d=DM)

        sc = [stack.enter_context(nc.psum_tensor(f"sc{i}", [P, 512], F32)) for i in range(UNROLL)]
        mxb = [stack.enter_context(nc.psum_tensor(f"mxb{i}", [P, 512], F32)) for i in range(2)]
        acc = stack.enter_context(nc.psum_tensor("acc", [P, 2, 512], F32))
        bank = stack.enter_context(nc.psum_tensor("bank", [P, 512], F32))
        bankb = bank[:, :].bitcast(BF16)

        load_x = sem("load_x")
        load_w = sem("load_w")
        load_g = sem("load_g")
        load_ctx = sem("load_ctx")
        load_late = sem("load_late")
        load_bias = sem("load_bias")
        stored = sem("stored")
        ident_ready = sem("ident_ready")
        power_ready = sem("power_ready")
        ones_ready = sem("ones_ready")
        zeros_ready = sem("zeros_ready")
        wsplit = sem("wsplit")
        pool_w = sem("pool_w")
        ln_step = sem("ln_step")
        xT_ready = sem("xT_ready")
        xT_hi = sem("xT_hi")
        xT_lo = sem("xT_lo")
        wT_ready = sem("wT_ready")
        wT_kept = sem("wT_kept")
        cT_ready = sem("cT_ready")
        cT_hi = sem("cT_hi")
        cT_lo = sem("cT_lo")
        v_ready = sem("v_ready")
        v_hi = sem("v_hi")
        v_lo = sem("v_lo")
        gate_step = sem("gate_step")

        bank_ready = sem("bank_ready")
        bank_hi = sem("bank_hi")
        bank_free = sem("bank_free")
        mx_ready = sem("mx_ready")
        mx_taken = sem("mx_taken")
        max_step = sem("max_step")
        sc_ready = sem("sc_ready")
        p_ready = sem("p_ready")
        lo_dve = sem("lo_dve")
        lo_pool = sem("lo_pool")
        pv_done = sem("pv_done")
        acc_taken = sem("acc_taken")
        fin_step = sem("fin_step")
        y_rows = sem("y_rows")
        x1_step = sem("x1_step")
        xn2_ready = sem("xn2_ready")
        xn2_kept = sem("xn2_kept")
        gate_ready = sem("gate_ready")
        gate_done = sem("gate_done")
        cell_step = sem("cell_step")
        o_ready = sem("o_ready")
        h_done = sem("h_done")
        h_rows = sem("h_rows")
        res_done = sem("res_done")

        def base(h, first, last):
            return BASE_0 if first else BASE_LAST if last else (h - 1) * PER_HEAD + BASE_1

        def use(h, first, last, half, what, i=0):
            at = (0 if half == 0 else len(bank_uses(first, last, 0))) + bank_uses(first, last, half).index(what)
            return base(h, first, last) + (at + i)

        def over_heads(eng, body):
            body(0, 0, True, False)
            with eng.Fori(0, (HEADS - 2) // 2) as pair:
                body(pair * 2 + 1, 1, False, False)
                body(pair * 2 + 2, 0, False, False)
            body(HEADS - 1, 1, False, True)

        block = stack.enter_context(nc.Block())

        @block.sync
        def _(sp):
            sp.dma_start(x_raw, x[0].rearrange("(n p) d -> p n d", p=P)).then_inc(load_x, 16)
            sp.dma_start(Wk_raw, Wk).then_inc(load_w, 16)
            sp.dma_start(Wq_raw, Wq).then_inc(load_w, 16)
            keys = ctx_768[0, 0:WHOLE * P].rearrange("(p t) c -> p t c", p=P)
            half = WHOLE // 2
            sp.dma_start(ctx_raw[:, 0:half, :], keys[:, 0:half, :]).then_inc(load_ctx, 16)
            sp.dma_start(ctx_raw[0:LAST, WHOLE, :], ctx_768[0, WHOLE * P:NKV]).then_inc(load_ctx, 16)
            sp.dma_start(ctx_raw[LAST:P, WHOLE, :], ctx_768[0, 0:P - LAST]).then_inc(load_ctx, 16)
            sp.dma_start(Wv_raw, Wv).then_inc(load_w, 16)
            for a in range(2):
                sp.dma_start(Wo_raw[a * DH:(a + 1) * DH, :].rearrange("p (h c) -> p h c", h=HEADS),
                             Wo.rearrange("(h p) c -> p h c", p=DH)).then_inc(load_w, 16)
            sp.wait_ge(bank_free, use(HEADS - 2, False, False, 1, ("minus_max", 1)) + 1)
            sp.dma_start(x_late, x[0].rearrange("(n p) d -> p n d", p=P)).then_inc(load_late, 16)
            for half in range(HALVES):
                sp.wait_ge(res_done, half + 1)
                sp.dma_start(out[0].rearrange("(n p) d -> p n d", p=P)[:, half * QT:(half + 1) * QT, :],
                             res[:, half * QT:(half + 1) * QT, :]).then_inc(stored, 16)
            sp.wait_ge(stored, 16 * HALVES)

        @block.gpsimd
        def _(pool):
            def inverse_root(n0, n1, step, v):
                pool.wait_ge(step, v + 6)
                pool.wait_ge(power_ready, 1)
                pool.tensor_tensor(stat[:, 1, n0:n1], stat[:, 2, n0:n1], stat[:, 3, n0:n1],
                                   ALU.pow).then_inc(step, 1)

            pool.memset(stat[:, 3, :], -0.5).then_inc(power_ready, 1)
            pool.memset(ident[:, :], 0.0).then_inc(ident_ready, 1)
            pool.wait_ge(ident_ready, 1)
            nc.gpsimd.affine_select(out=ident[:, :], in_=ident[:, :], compare_op=ALU.not_equal, fill=1.0,
                                    base=0, pattern=[[-1, P]], channel_multiplier=1).then_inc(ident_ready, 1)
            pool.wait_ge(ident_ready, 2)
            pool.tensor_copy(identb[:, :], ident[:, :]).then_inc(ident_ready, 1)
            inverse_root(0, NQ // P, ln_step, 0)
            pool.wait_ge(load_w, 80)
            pool.tensor_copy(Wv_hi[:, :], Wv_raw).then_inc(pool_w, 1)
            pool.tensor_copy(Wo_hi[:, :], Wo_raw).then_inc(pool_w, 1)
            pool.wait_ge(pool_w, 2)
            pool.tensor_tensor(Wv_lo[:, :], Wv_raw, Wv_hi[:, :], ALU.subtract).then_inc(pool_w, 1)
            pool.tensor_tensor(Wo_lo[:, :], Wo_raw, Wo_hi[:, :], ALU.subtract).then_inc(pool_w, 1)
            pool.wait_ge(pool_w, 4)
            pool.wait_ge(cT_ready, TURNS)
            pool.wait_ge(wT_ready, 4)
            pool.wait_ge(wsplit, 4)
            pool.wait_ge(gate_step, 4)
            pool.wait_ge(xT_ready, 2)
            pool.memset(V4[:, 0:WHOLE, :, DH], 1.0).then_inc(ones_ready, 1)

            def low_part(n, j):
                pool.wait_ge(p_ready, n + 1)
                hi = prob[:, j, :].bitcast(BF16).rearrange("p (q two) -> p q two", two=2)[:, :, 1]
                pool.tensor_tensor(prob_lo[:, j, 0:POOL_COLS], prob[:, j, 0:POOL_COLS], hi[:, 0:POOL_COLS],
                                   ALU.subtract).then_inc(lo_pool, 1)

            with pool.Fori(0, HEADS * HALVES * TILES, UNROLL) as n:
                for j in range(UNROLL):
                    low_part(n + j, j)
            for half in range(HALVES):
                inverse_root(half * QT, (half + 1) * QT, x1_step, (1 + LN_STEPS) * half + 1)

        @block.tensor
        def _(pe):
            def take_bank(n):
                pe.wait_ge(bank_free, n)

            pe.wait_ge(ident_ready, 2)
            pe.wait_ge(load_w, 80)
            for n in range(2):
                for k in range(4):
                    h = 4 * n + k
                    m = pe.transpose(sc[n][0:DH, k * DC:(k + 1) * DC], Wk_raw[:, h * DH:(h + 1) * DH],
                                     ident[0:DC, 0:DC])
                m.then_inc(wT_ready, 1)
            pe.wait_ge(ln_step, LN_STEPS)
            for n in range(HALVES):
                for k in range(QT):
                    m = pe.transpose(acc[:, n, k * P:(k + 1) * P], x_raw[:, n * QT + k, :], ident[:, :])
                m.then_inc(xT_ready, 1)

            def context_turn(i, b, wait):
                if wait is not None:
                    pe.wait_ge(cT_lo, wait)
                for j in range(UNROLL):
                    off = (i * UNROLL + j) * DC
                    m = pe.transpose(mxb[b][0:DC, j * P:(j + 1) * P], raw[:, off:off + DC], ident[:, :])
                m.then_inc(cT_ready, 1)

            pe.wait_ge(load_ctx, 64)
            for i in range(TURNS):
                context_turn(i, i % 2, i - 1 if i >= 2 else None)

            pe.wait_ge(load_g, 13 * 16)
            pe.wait_ge(wT_kept, 2)
            for n in range(5):
                b = sc[0] if n < 4 else sc[1]
                m = pe.transpose(b[:, (n % 4) * P:(n % 4 + 1) * P], gate_raw[:, [0, 1, 2, 6, 7][n], :], ident[:, :])
                if n >= 3:
                    m.then_inc(wT_ready, 1)

            def q_part(head, half, n):
                take_bank(n)
                s = slice(half * QG, (half + 1) * QG)
                whi = WqD_hi[:, :, :, :].rearrange("p h a d -> p (h a d)")[:, ds(head * P, P)]
                wlo = WqD_lo[:, :, :, :].rearrange("p h a d -> p (h a d)")[:, ds(head * P, P)]
                pe.matmul(bank[:, :], whi, xnT_hi[:, s], start=True, stop=False)
                pe.matmul(bank[:, :], wlo, xnT_hi[:, s], start=False, stop=False)
                pe.matmul(bank[:, :], whi, xnT_lo[:, s], start=False, stop=True).then_inc(bank_ready, 1)

            def q_low_part(head, n):
                take_bank(n)
                pe.matmul(bank[0:DC, :], WkT[:, ds(head * DC, DC)], q_low[:, :], start=True,
                          stop=True).then_inc(bank_ready, 1)

            def k_part(head, i, n):
                take_bank(n)
                whi = WkD_hi[:, :, :, :].rearrange("p h a d -> p (h a d)")[:, ds(head * P, P)]
                wlo = WkD_lo[:, :, :, :].rearrange("p h a d -> p (h a d)")[:, ds(head * P, P)]
                chi = ctx_hi[0:DC, ds(i * CHUNK, CHUNK)]
                clo = ctx_lo[0:DC, ds(i * CHUNK, CHUNK)]
                pe.matmul(bank[:, 0:CHUNK], whi, chi, start=True, stop=False)
                pe.matmul(bank[:, 0:CHUNK], wlo, chi, start=False, stop=False)
                pe.matmul(bank[:, 0:CHUNK], whi, clo, start=False, stop=True).then_inc(bank_ready, 1)

            def max_product(par, half, i, qt, m):
                if m is not None:
                    pe.wait_ge(mx_taken, m - 1)
                q = half * QG + qt * P
                pe.matmul(mxb[qt % 2][:, 0:CHUNK], qA[:, par, q:q + P], K[:, ds(par * KEYS + i * CHUNK, CHUNK)],
                          start=True, stop=True).then_inc(mx_ready, 1)

            pe.wait_ge(xT_lo, 2)
            pe.wait_ge(wsplit, 4)
            pe.wait_ge(zeros_ready, 2)
            for half in range(HALVES):
                q_part(0, half, 2 * half)
                q_low_part(0, 2 * half + 1)
            pe.wait_ge(cT_lo, TURNS)
            with pe.Fori(0, TURNS) as i:
                k_part(0, i, i + 4)
            take_bank(len(PRO_USES))
            pe.wait_ge(pool_w, 4)
            pe.wait_ge(wT_kept, 4)
            pe.wait_ge(ones_ready, 1)

            def v_turn(i, first):
                for j in range(UNROLL):
                    if not first:
                        pe.wait_ge(v_lo, i * UNROLL + j - 2)
                    chi = ctx_hi[0:DC, ds((i * UNROLL + j) * P, P)]
                    clo = ctx_lo[0:DC, ds((i * UNROLL + j) * P, P)]
                    pe.matmul(sc[j][:, :], chi, Wv_hi[:, :], start=True, stop=False)
                    pe.matmul(sc[j][:, :], chi, Wv_lo[:, :], start=False, stop=False)
                    pe.matmul(sc[j][:, :], clo, Wv_hi[:, :], start=False, stop=True).then_inc(v_ready, 1)
                    for qt in [(0, 1), (2, 3), ()][j]:
                        max_product(0, 0, i, qt, None if first and qt < 2 else i * QT + qt)

            v_turn(0, True)
            with pe.Fori(1, TURNS) as i:
                v_turn(i, False)

            def group_turn(h, par, half, first, last, i, opening):
                g = h * HALVES + half
                n0 = g * TILES + i * UNROLL
                more = not (last and half == 1)
                npar, nhalf = (par, 1) if half == 0 else (1 - par, 0)
                start = first and half == 0 and opening
                q = slice(half * QG, (half + 1) * QG)

                def u(what, i=0):
                    return use(h, first, last, half, what, i)

                for j in range(UNROLL):
                    n = n0 + j
                    if not start:
                        pe.wait_ge(p_ready, n - 2)
                    if opening and first and half == 0 and j == 0:
                        pe.wait_ge(v_lo, TILES)
                    tile = ds(par * KEYS + (i * UNROLL + j) * P, P)
                    pe.matmul(sc[j][:, :], K[:, tile], qA[:, par, q], start=True, stop=False)
                    if opening and j == 0:
                        take_bank(u(("minus_max", half)))
                        pe.wait_ge(max_step, g * 3 + 3)
                        for qt in range(QT):
                            m = pe.transpose(bankb[0:2, qt * P:(qt + 1) * P], neg_max2[:, qt, :], identb[:, :])
                        m.then_inc(bank_ready, 1)
                    if more:
                        for qt in [(0, 1), (2, 3), ()][j]:
                            max_product(npar, nhalf, i, qt, (g + 1) * MX + i * QT + qt)
                    if opening and j == 0:
                        pe.wait_ge(bank_free, u(("minus_max", half)) + 1)
                    pe.matmul(sc[j][:, :], ctx_hi[0:AUG, ds((i * UNROLL + j) * P, P)], qB[0:AUG, par, q],
                              start=False, stop=True).then_inc(sc_ready, 1)
                    if j == 0 and half == 0 and not last:
                        k_part(h + 1, i, u(("K", 0)) if opening else u(("K", 1), i - 1))
                    if j == 1 and opening and not last:
                        q_part(h + 1, half, u(("QP", half)))
                    if not (start and j < 2):
                        back = opening and j < 2
                        hv = (h if half == 1 else h - 1) if back else h
                        tv = TILES - 2 + j if back else i * UNROLL + j - 2
                        p_times_v(hv, tv, n - 2, (j - 2) % UNROLL, opening and j == 2, g)
                    if opening and j == 0 and not first:
                        out_product(h - 1, u(("Y", half)))
                    if opening and j == 2 and not last:
                        q_low_part(h + 1, u(("QL", half)))

            def p_times_v(hv, tv, n, slot, begin, g):
                pe.wait_ge(p_ready, n + 1)
                pe.wait_ge(lo_dve, n + 1)
                pe.wait_ge(lo_pool, n + 1)
                if begin and not (isinstance(g, int) and g == 0):
                    pe.wait_ge(acc_taken, g)
                hi = prob[:, slot, :].bitcast(BF16).rearrange("p (q two) -> p q two", two=2)[:, :, 1]
                off = tv * (HEADS * VW) + hv * VW
                for qt in range(QT):
                    o = acc[:, qt // 2, (qt % 2) * VW:(qt % 2 + 1) * VW]
                    pe.matmul(o, hi[:, qt * P:(qt + 1) * P], V[:, ds(off, VW)], start=begin and qt % 2 == 0,
                              stop=False, skip_group_check=True)
                for qt in range(QT):
                    o = acc[:, qt // 2, (qt % 2) * VW:(qt % 2) * VW + DH + 1]
                    m = pe.matmul(o, prob_lo[:, slot, qt * P:(qt + 1) * P], V[:, ds(off, DH + 1)], start=False,
                                  stop=True, skip_group_check=True)
                m.then_inc(pv_done, 1)

            def turn_heads(g1, n):
                take_bank(n)
                pe.wait_ge(fin_step, g1 * 3)
                for k in range(QT // 2):
                    m = pe.transpose(bank[:, k * P:(k + 1) * P],
                                     o_norm[:, 2 * k:2 * k + 2, :].rearrange("p a d -> p (a d)"), ident[:, :])
                m.then_inc(bank_ready, 1)

            def out_product(head, n):
                take_bank(n)
                pe.matmul(bank[:, :], Wo_hi[:, ds(head * DM, DM)], oT[:, :], start=True, stop=False)
                pe.matmul(bank[:, :], Wo_lo[:, ds(head * DM, DM)], oT[:, :], start=False,
                          stop=True).then_inc(bank_ready, 1)

            def head_body(h, par, first, last):
                for half in range(HALVES):
                    group_turn(h, par, half, first, last, 0, True)
                    with pe.Fori(1, TURNS) as i:
                        group_turn(h, par, half, first, last, i, False)
                    if not (first and half == 0):
                        turn_heads(h * HALVES + half, use(h, first, last, half, ("OT", half)))

            over_heads(pe, head_body)
            n_last = HEADS * HALVES * TILES
            for j in range(2):
                p_times_v(HEADS - 1, TILES - 2 + j, n_last - 2 + j, (TILES - 2 + j) % UNROLL, False, 1)
            out_product(HEADS - 1, BASE_TAIL)
            turn_heads(HEADS * HALVES, BASE_TAIL + 1)
            out_product(HEADS - 1, BASE_TAIL + 2)

            for half in range(HALVES):
                pe.wait_ge(bank_free, BASE_TAIL + 1 + 2 * half)
                pe.wait_ge(p_ready, n_last)
                for k in range(QT):
                    c = (half * QT + k) * P
                    m = pe.transpose(sc[half][:, k * P:(k + 1) * P], yT[:, c:c + P], ident[:, :])
                m.then_inc(y_rows, 1)
            for half in range(HALVES):
                s = slice(half * QG, (half + 1) * QG)
                pe.wait_ge(x1_step, (1 + LN_STEPS) * (half + 1))
                for k in range(QT):
                    m = pe.transpose(mxb[half][:, k * P:(k + 1) * P], xc[:, half * QT + k, :], ident[:, :])
                m.then_inc(xn2_ready, 1)
                pe.wait_ge(xn2_kept, half + 1)
                for w, b in enumerate([sc[2][:, :], acc[:, 0, :], acc[:, 1, :]]):
                    if half == 0 and w == 1:
                        pe.wait_ge(acc_taken, HEADS * HALVES)
                    if half == 1:
                        pe.wait_ge(gate_done, w + 1)
                    pe.matmul(b, gateT[:, w, :], xn2T[:, s], start=True, stop=True).then_inc(gate_ready, 1)
            for half in range(HALVES):
                s = slice(half * QG, (half + 1) * QG)
                pe.matmul(sc[half][:, :], gateT[:, 3, :], xn2T[:, s], start=True, stop=False)
                pe.wait_ge(cell_step, 3 * (half + 1))
                pe.matmul(sc[half][:, :], gateT[:, 4, :], cT[:, s], start=False, stop=True).then_inc(o_ready, 1)
            for half in range(HALVES):
                pe.wait_ge(h_done, half + 1)
                for k in range(QT):
                    c = (half * QT + k) * P
                    m = pe.transpose(mxb[half][:, k * P:(k + 1) * P], hT[:, c:c + P], ident[:, :])
                m.then_inc(h_rows, 1)

        @block.scalar
        def _(act):
            keys = ctx_768[0, 0:WHOLE * P].rearrange("(p t) c -> p t c", p=P)
            half = WHOLE // 2
            act.dma_start(ctx_raw[:, half:WHOLE, :], keys[:, half:WHOLE, :]).then_inc(load_ctx, 16)
            for n, w in enumerate([wf, wi, wc, uf, ui, uc, wo, uo]):
                act.dma_start(gate_raw[:, n, :], w).then_inc(load_g, 16)
            for n, w in enumerate([bf, bi, bc]):
                act.dma_start(cols[:, n:n + 1], w.rearrange("(p a) -> p a", a=1)).then_inc(load_g, 16)
            act.dma_start(cols[:, 5:6], in_c.rearrange("(p a) -> p a", a=1)).then_inc(load_g, 16)
            act.dma_start(cbc, in_c.rearrange("(a d) -> a d", a=1).broadcast_to([P, P])).then_inc(load_g, 16)
            act.dma_start(cols[:, 3:4], fbo.rearrange("(p a) -> p a", a=1)).then_inc(load_bias, 16)
            act.dma_start(cols[:, 4:5], xbo.rearrange("(p a) -> p a", a=1)).then_inc(load_bias, 16)

            for n in range(2):
                act.wait_ge(wT_ready, n + 1)
                act.copy(WkT[0:DH, n * 4 * DC:(n + 1) * 4 * DC], sc[n][0:DH, 0:4 * DC]).then_inc(wT_kept, 1)
            for n in range(HALVES):
                act.wait_ge(xT_ready, n + 1)
                act.copy(xnT_hi[:, n * QG:(n + 1) * QG], acc[:, n, :]).then_inc(xT_hi, 1)
            for i in range(TURNS):
                act.wait_ge(cT_ready, i + 1)
                act.copy(ctx_hi[0:DC, i * CHUNK:(i + 1) * CHUNK], mxb[i % 2][0:DC, 0:CHUNK]).then_inc(cT_hi, 1)
            act.wait_ge(wT_ready, 3)
            act.copy(gateT[:, 0:4, :].rearrange("p a b -> p (a b)"), sc[0][:, :]).then_inc(wT_kept, 1)
            act.wait_ge(wT_ready, 4)
            act.copy(gateT[:, 4, :], sc[1][:, 0:P]).then_inc(wT_kept, 1)

            def q_high(par, half, n, nb):
                act.wait_ge(bank_ready, n + 1)
                act.copy(qA[:, par, half * QG:(half + 1) * QG], bank[:, :]).then_inc(bank_hi, 1)

            def q_low_out(par, half, n):
                act.wait_ge(bank_ready, n + 1)
                act.copy(qB[0:DC, par, half * QG:(half + 1) * QG], bank[0:DC, :]).then_inc(bank_free, 1)

            def k_high(par, i, n):
                act.wait_ge(bank_ready, n + 1)
                act.copy(K[:, ds(par * KEYS + i * CHUNK, CHUNK)], bank[:, 0:CHUNK]).then_inc(bank_hi, 1)

            for half in range(HALVES):
                q_high(0, half, 2 * half, None)
                q_low_out(0, half, 2 * half + 1)
            with act.Fori(0, TURNS) as i:
                k_high(0, i, i + 4)
            act.wait_ge(ones_ready, 4)

            def v_high(t, b, rows):
                act.wait_ge(v_ready, t + 1)
                off = t * HEADS * VW
                dst = V[0:rows, ds(off, HEADS * VW)].rearrange("p (h c) -> p h c", h=HEADS)[:, :, 0:DH]
                act.copy(dst, sc[b][0:rows, :].rearrange("p (h c) -> p h c", h=HEADS)).then_inc(v_hi, 1)

            with act.Fori(0, TURNS - 1) as i:
                for j in range(UNROLL):
                    v_high(i * UNROLL + j, j, P)
            for j in range(UNROLL):
                t = TILES - UNROLL + j
                v_high(t, j, P if t < WHOLE else LAST)

            def exp_tile(n, j, fresh):
                act.wait_ge(sc_ready, n + 1)
                if not fresh:
                    act.wait_ge(pv_done, n - 2)
                act.activation(prob[:, j, :], sc[j][:, :], ACT.Exp, scale=SCALE).then_inc(p_ready, 1)

            def group_turn(h, par, half, first, last, i, opening):
                g = h * HALVES + half
                n0 = g * TILES + i * UNROLL
                start = first and half == 0 and opening

                def u(what, i=0):
                    return use(h, first, last, half, what, i)

                for j in range(UNROLL):
                    if opening and j == 0:
                        act.wait_ge(bank_ready, u(("minus_max", half)) + 1)
                        act.copy(qB[DC:AUG, par, half * QG:(half + 1) * QG], bankb[0:2, 0:QG]).then_inc(bank_free, 1)
                    exp_tile(n0 + j, j, start)
                    if j == 0 and half == 0 and not last:
                        k_high(1 - par, i, u(("K", 0)) if opening else u(("K", 1), i - 1))
                    if j == 1 and opening and not last:
                        q_high(1 - par, half, u(("QP", half)), None)
                    if j == 1 and opening and not start:
                        take_sums(g, n0)
                    if j == 2 and opening and not last:
                        q_low_out(1 - par, half, u(("QL", half)))

            def take_sums(g, n):
                act.wait_ge(pv_done, n)
                if not (isinstance(g, int) and g == 1):
                    act.wait_ge(fin_step, (g - 1) * 3)
                act.copy(acc_raw[:, :, :].rearrange("p (b t) c -> p b (t c)", b=2),
                         acc[:, :, 0:2 * VW]).then_inc(acc_taken, 1)

            def heads_high(n):
                act.wait_ge(bank_ready, n + 1)
                act.copy(oT4[0:DH, :, 0, :], bank[0:DH, 0:2 * P].rearrange("p (k q) -> p k q", k=2))
                act.copy(oT4[0:DH, :, 1, :], bank[DH:P, 0:2 * P].rearrange("p (k q) -> p k q", k=2)
                         ).then_inc(bank_hi, 1)

            def head_body(h, par, first, last):
                for half in range(HALVES):
                    group_turn(h, par, half, first, last, 0, True)
                    with act.Fori(1, TURNS) as i:
                        group_turn(h, par, half, first, last, i, False)
                    if not (first and half == 0):
                        heads_high(use(h, first, last, half, ("OT", half)))

            over_heads(act, head_body)
            take_sums(HEADS * HALVES, HEADS * HALVES * TILES)
            heads_high(BASE_TAIL + 1)

            act.wait_ge(pv_done, HEADS * HALVES * TILES)
            act.wait_ge(gate_step, 5)
            for half in range(HALVES):
                s = slice(half * QG, (half + 1) * QG)
                act.wait_ge(xn2_ready, half + 1)
                act.copy(xn2T[:, s], mxb[half][:, :]).then_inc(xn2_kept, 1)
                for w, (dst, fn) in enumerate([(fT, ACT.Sigmoid), (iT, ACT.Sigmoid), (gT, ACT.Tanh)]):
                    act.wait_ge(gate_ready, 3 * half + w + 1)
                    b = sc[2][:, :] if w == 0 else acc[:, w - 1, :]
                    act.activation(dst[:, s], b, fn, bias=gate_bias[:, w:w + 1]).then_inc(gate_done, 1)
            for half in range(HALVES):
                s = slice(half * QG, (half + 1) * QG)
                act.wait_ge(o_ready, half + 1)
                act.activation(hT[:, s], sc[half][:, :], ACT.Tanh, bias=cols[:, 3:4]).then_inc(h_done, 1)

        @block.vector
        def _(dve):
            def layer_norm(src, dst, sq, n0, n1, sem_, v):
                n = n1 - n0
                mean, var = stat[:, 0, n0:n1], stat[:, 1, n0:n1]
                nrm = stat[:, 2, n0:n1]
                dve.tensor_reduce(mean, src[:, n0:n1, :], AX.X, ALU.add).then_inc(sem_, 1)
                dve.wait_ge(sem_, v + 1)
                dve.tensor_scalar(mean, mean, 1.0 / DM, None, ALU.mult).then_inc(sem_, 1)
                dve.wait_ge(sem_, v + 2)
                dve.tensor_tensor(dst[:, n0:n1, :], src[:, n0:n1, :],
                                  mean.rearrange("p (n a) -> p n a", a=1).broadcast_to([P, n, DM]),
                                  ALU.subtract).then_inc(sem_, 1)
                dve.wait_ge(sem_, v + 3)
                dve.tensor_tensor(sq[:, n0:n1, :], dst[:, n0:n1, :], dst[:, n0:n1, :], ALU.mult).then_inc(sem_, 1)
                dve.wait_ge(sem_, v + 4)
                dve.tensor_reduce(var, sq[:, n0:n1, :], AX.X, ALU.add).then_inc(sem_, 1)
                dve.wait_ge(sem_, v + 5)
                dve.tensor_scalar(nrm, var, 1.0 / DM, EPS, ALU.mult, ALU.add).then_inc(sem_, 1)
                dve.wait_ge(sem_, v + 6)
                dve.wait_ge(sem_, v + 7)
                dve.tensor_tensor(dst[:, n0:n1, :], dst[:, n0:n1, :],
                                  var.rearrange("p (n a) -> p n a", a=1).broadcast_to([P, n, DM]),
                                  ALU.mult).then_inc(sem_, 1)

            dve.memset(q_low[DH:P, :], 0.0).then_inc(zeros_ready, 1)
            dve.memset(WkT[DH:P, :], 0.0).then_inc(zeros_ready, 1)
            dve.memset(ctx_hi[DC:AUG, :], 1.0).then_inc(ones_ready, 1)
            dve.memset(V4[:, WHOLE, :, :], 0.0).then_inc(ones_ready, 1)
            dve.wait_ge(ones_ready, 2)
            dve.memset(V4[0:LAST, WHOLE, :, DH], 1.0).then_inc(ones_ready, 1)
            dve.wait_ge(load_x, 16)
            layer_norm(x_raw, x_raw, x_sq, 0, 8, ln_step, 0)
            dve.wait_ge(load_w, 80)
            for n, (w, hi) in enumerate([(Wk_raw, WkD_hi), (Wq_raw, WqD_hi)]):
                m = w.shape[0]
                for a in range(2):
                    ins = dve.tensor_copy(hi[0:m, :, a, :], w.rearrange("p (h d) -> p h d", h=HEADS))
                ins.then_inc(wsplit, 1)
            dve.wait_ge(wsplit, 2)
            for n, (w, hi, lo) in enumerate([(Wk_raw, WkD_hi, WkD_lo), (Wq_raw, WqD_hi, WqD_lo)]):
                m = w.shape[0]
                for a in range(2):
                    ins = dve.tensor_tensor(lo[0:m, :, a, :], w.rearrange("p (h d) -> p h d", h=HEADS),
                                            hi[0:m, :, 0, :], ALU.subtract)
                ins.then_inc(wsplit, 1)
            for n in range(HALVES):
                dve.wait_ge(xT_hi, n + 1)
                s = slice(n * QG, (n + 1) * QG)
                dve.tensor_tensor(xnT_lo[:, s], acc[:, n, :], xnT_hi[:, s], ALU.subtract).then_inc(xT_lo, 1)
            for i in range(TURNS):
                dve.wait_ge(cT_hi, i + 1)
                s = slice(i * CHUNK, (i + 1) * CHUNK)
                dve.tensor_tensor(ctx_lo[0:DC, s], mxb[i % 2][0:DC, 0:CHUNK], ctx_hi[0:DC, s],
                                  ALU.subtract).then_inc(cT_lo, 1)
            dve.wait_ge(load_g, 13 * 16)
            for w in range(3):
                dve.tensor_tensor(gsum[:, w, :], gate_raw[:, 3 + w, :], cbc, ALU.mult).then_inc(gate_step, 1)
            dve.wait_ge(gate_step, 3)
            dve.tensor_reduce(gate_bias[:, :], gsum, AX.X, ALU.add).then_inc(gate_step, 1)
            dve.wait_ge(gate_step, 4)
            dve.tensor_tensor(gate_bias[:, :], gate_bias[:, :], cols[:, 0:3], ALU.add).then_inc(gate_step, 1)
            dve.wait_ge(load_bias, 32)
            dve.memset(yT[:, :], 0.0).then_inc(gate_step, 1)
            dve.wait_ge(gate_step, 6)
            dve.tensor_scalar(yT[:, :], yT[:, :], cols[:, 4:5], None, ALU.add).then_inc(gate_step, 1)

            def q_low_dve(par, half, n, nh):
                dve.wait_ge(bank_hi, nh)
                dve.tensor_tensor(q_low[0:DH, :], bank[0:DH, :], qA[0:DH, par, half * QG:(half + 1) * QG],
                                  ALU.subtract).then_inc(bank_free, 1)

            def k_low(par, i, nh):
                dve.wait_ge(bank_hi, nh)
                k = K[DH:P, ds(par * KEYS + i * CHUNK, CHUNK)]
                dve.tensor_tensor(k, bank[DH:P, 0:CHUNK], k, ALU.subtract).then_inc(bank_free, 1)

            def hand(uses, what, half=None):
                n = 0
                for k in uses:
                    if k[0] in ("QP", "K", "OT"):
                        n += 1
                    if k == what:
                        return n
                return n

            for half in range(HALVES):
                q_low_dve(0, half, 0, half + 1)
            with dve.Fori(0, TURNS) as i:
                k_low(0, i, i + 3)
            hb0 = 2 + TURNS
            hb1 = hb0 + hand(head_uses(True, False), None)
            per = hand(head_uses(False, False), None)
            hbl = hb1 + (HEADS - 2) * per
            hbt = hbl + hand(head_uses(False, True), None)

            def hands(h, first, last, half, what):
                b = hb0 if first else hbl if last else (h - 1) * per + hb1
                if half == 1:
                    b = b + hand(bank_uses(first, last, 0), None)
                return b + hand(bank_uses(first, last, half), what)

            def reduce_max(i, qt, m, fresh):
                if fresh is not None:
                    dve.wait_ge(max_step, fresh)
                dve.wait_ge(mx_ready, m + 1)
                dve.tensor_reduce(part_max[:, qt, ds(i, 1)], mxb[qt % 2][:, 0:CHUNK], AX.X,
                                  ALU.max).then_inc(mx_taken, 1)

            def minus_max(g1):
                dve.wait_ge(mx_taken, g1 * MX)
                if not (isinstance(g1, int) and g1 == 1):
                    dve.wait_ge(max_step, (g1 - 1) * 3)
                dve.tensor_reduce(neg_max[:, :], part_max[:, :, :], AX.X, ALU.max, negate=True).then_inc(max_step, 1)
                dve.wait_ge(max_step, (g1 - 1) * 3 + 1)
                dve.tensor_copy(neg_max2[:, :, 0], neg_max[:, :]).then_inc(max_step, 1)
                dve.wait_ge(max_step, (g1 - 1) * 3 + 2)
                dve.tensor_tensor(neg_max2[:, :, 1], neg_max[:, :], neg_max2[:, :, 0],
                                  ALU.subtract).then_inc(max_step, 1)

            def v_low(t, b, rows):
                dve.wait_ge(v_hi, t + 1)
                v = V[0:rows, ds(t * HEADS * VW, HEADS * VW)].rearrange("p (h c) -> p h c", h=HEADS)
                dve.tensor_tensor(v[:, :, DH + 1:VW], sc[b][0:rows, :].rearrange("p (h c) -> p h c", h=HEADS),
                                  v[:, :, 0:DH], ALU.subtract).then_inc(v_lo, 1)

            def v_turn(i, last):
                for j in range(UNROLL):
                    t = i * UNROLL + j
                    v_low(t, j, LAST if last and j == UNROLL - 1 else P)
                    for qt in [(0, 1), (2, 3), ()][j]:
                        reduce_max(i, qt, i * QT + qt, None)

            dve.wait_ge(ones_ready, 4)
            with dve.Fori(0, TURNS - 1) as i:
                v_turn(i, False)
            v_turn(TURNS - 1, True)
            minus_max(1)
            def low_part(n, j):
                dve.wait_ge(p_ready, n + 1)
                hi = prob[:, j, :].bitcast(BF16).rearrange("p (q two) -> p q two", two=2)[:, :, 1]
                dve.tensor_tensor(prob_lo[:, j, POOL_COLS:QG], prob[:, j, POOL_COLS:QG], hi[:, POOL_COLS:QG],
                                  ALU.subtract).then_inc(lo_dve, 1)

            def add_output(half, n):
                dve.wait_ge(bank_ready, n + 1)
                y = yT[:, half * QG:(half + 1) * QG]
                dve.tensor_tensor(y, bank[:, :], y, ALU.add).then_inc(bank_free, 1)

            def divide(g1):
                dve.wait_ge(acc_taken, g1)
                dve.reciprocal(rden[:, :], acc_raw[:, :, DH]).then_inc(fin_step, 1)
                dve.tensor_tensor(o_norm[:, :, :], acc_raw[:, :, 0:DH], acc_raw[:, :, DH + 1:VW],
                                  ALU.add).then_inc(fin_step, 1)
                dve.wait_ge(fin_step, (g1 - 1) * 3 + 2)
                dve.tensor_tensor(o_norm[:, :, :], o_norm[:, :, :],
                                  rden[:, :].rearrange("p (n a) -> p n a", a=1).broadcast_to([P, QT, DH]),
                                  ALU.mult).then_inc(fin_step, 1)

            def heads_low(nh):
                dve.wait_ge(bank_hi, nh)
                for a in range(2):
                    m = dve.tensor_tensor(oT4[DH:P, :, a, :],
                                          bank[a * DH:(a + 1) * DH, 0:2 * P].rearrange("p (k q) -> p k q", k=2),
                                          oT4[0:DH, :, a, :], ALU.subtract)
                m.then_inc(bank_free, 1)

            def group_turn(h, par, half, first, last, i, opening):
                g = h * HALVES + half
                n0 = g * TILES + i * UNROLL
                more = not (last and half == 1)
                start = first and half == 0 and opening

                def u(what, i=0):
                    return use(h, first, last, half, what, i)

                for j in range(UNROLL):
                    if not (start and j == 0):
                        low_part(n0 + j - 1, (j - 1) % UNROLL)
                    if more:
                        for qt in [(0, 1), (2, 3), ()][j]:
                            reduce_max(i, qt, (g + 1) * MX + i * QT + qt, g * 3 + 1 if opening else None)
                    if j == 0 and half == 0 and not last:
                        nh = hands(h, first, last, half, ("K", 0)) if opening else \
                            hands(h, first, last, half, ("K", 1)) + (i - 1)
                        k_low(1 - par, i, nh)
                    if j == 0 and opening and not first:
                        add_output(half, u(("Y", half)))
                    if j == 1 and opening and not last:
                        q_low_dve(1 - par, half, 0, hands(h, first, last, half, ("QP", half)))
                    if j == 2 and opening and not start:
                        divide(g)

            def head_body(h, par, first, last):
                for half in range(HALVES):
                    group_turn(h, par, half, first, last, 0, True)
                    with dve.Fori(1, TURNS) as i:
                        group_turn(h, par, half, first, last, i, False)
                    if not (last and half == 1):
                        minus_max(h * HALVES + half + 2)
                    if not (first and half == 0):
                        heads_low(hands(h, first, last, half, ("OT", half)))

            over_heads(dve, head_body)
            n_last = HEADS * HALVES * TILES
            low_part(n_last - 1, (TILES - 1) % UNROLL)
            add_output(0, BASE_TAIL)
            divide(HEADS * HALVES)
            heads_low(hbt + 1)
            add_output(1, BASE_TAIL + 2)

            dve.wait_ge(load_late, 16)
            dve.wait_ge(pv_done, n_last)
            for half in range(HALVES):
                a, b = half * QT, (half + 1) * QT
                dve.wait_ge(y_rows, half + 1)
                dve.tensor_tensor(x1[:, a:b, :], sc[half][:, :].rearrange("p (n d) -> p n d", d=DM),
                                  x_late[:, a:b, :], ALU.add).then_inc(x1_step, 1)
                dve.wait_ge(x1_step, (1 + LN_STEPS) * half + 1)
                layer_norm(x1, xc, sq2, a, b, x1_step, (1 + LN_STEPS) * half + 1)
            for half in range(HALVES):
                s = slice(half * QG, (half + 1) * QG)
                dve.wait_ge(gate_done, 3 * (half + 1))
                dve.tensor_scalar(fT[:, s], fT[:, s], cols[:, 5:6], None, ALU.mult).then_inc(cell_step, 1)
                dve.tensor_tensor(iT[:, s], iT[:, s], gT[:, s], ALU.mult).then_inc(cell_step, 1)
                dve.wait_ge(cell_step, 3 * half + 2)
                dve.tensor_tensor(cT[:, s], fT[:, s], iT[:, s], ALU.add).then_inc(cell_step, 1)
            for half in range(HALVES):
                a, b = half * QT, (half + 1) * QT
                dve.wait_ge(h_rows, half + 1)
                dve.tensor_tensor(res[:, a:b, :], mxb[half][:, :].rearrange("p (n d) -> p n d", d=DM),
                                  x1[:, a:b, :], ALU.add).then_inc(res_done, 1)


_INS = ["x", "ctx_768", "L0_xattn_Wq", "L0_xattn_Wk", "L0_xattn_Wv", "L0_xattn_Wo", "L0_xattn_bo",
        "L0_ffn_wf", "L0_ffn_uf", "L0_ffn_bf", "L0_ffn_wi", "L0_ffn_ui", "L0_ffn_bi",
        "L0_ffn_wc", "L0_ffn_uc", "L0_ffn_bc", "L0_ffn_wo", "L0_ffn_uo", "L0_ffn_bo", "L0_ffn_in_c"]


def kernel(**inputs):
    import numpy as _np
    import concourse.bacc as _bacc
    from concourse import mybir as _mybir
    from concourse.bass_utils import run_bass_kernel_spmd as _run

    nc = _bacc.Bacc("TRN2", target_bir_lowering=False, num_devices=1)
    arrays, args = {}, []
    for name in _INS:
        a = _np.ascontiguousarray(inputs[name])
        arrays[f"in_{name}_dram"] = a
        args.append(nc.dram_tensor(f"in_{name}_dram", a.shape, _mybir.dt.from_np(a.dtype), kind="ExternalInput").ap())
    out = nc.dram_tensor("out_0_dram", (1, NQ, DM), _mybir.dt.float32, kind="ExternalOutput").ap()
    build(nc, *args, out)
    r = _run(nc, [arrays], core_ids=[0])
    return r.results[0]["out_0_dram"]
```

```python
from contextlib import ExitStack

import numpy as np

import concourse.bass as bass
from concourse import mybir

F32 = mybir.dt.float32
BF16 = mybir.dt.bfloat16
ALU = mybir.AluOpType
ACT = mybir.ActivationFunctionType
AX = mybir.AxisListType
ds = bass.ds

P = 128
HEADS = 8
DH = 64
DM = 128
DC = 96
NQ = 1024
NKV = 6404
SCALE = DH ** -0.5
EPS = 1e-5

TILES = (NKV + P - 1) // P
WHOLE = NKV // P
LAST = NKV - WHOLE * P
UNROLL = 3
TURNS = TILES // UNROLL
CHUNK = UNROLL * P
QG = 512
QT = QG // P
HALVES = NQ // QG
VW = 2 * DH + 1
AUG = DC + 2
POOL_COLS = 320
KEYS = TILES * P
LAG = UNROLL
MAX_TURNS = TURNS - 1
MAX_KEYS = KEYS // MAX_TURNS
MX = MAX_TURNS * QT
CT = 8
GROUPS = -(-TILES // CT)
CTX_LOADS = [(0, 2 * CT), (2 * CT, 4 * CT), (4 * CT, WHOLE)]
LOOP_HALF_0 = [(2, TURNS - 1, 0)]
LOOP_HALF_1 = [(2, 5, TURNS - 3), (5, TURNS - 1, None)]
LOOP_LAST = [(2, TURNS - 1, None)]
KEY_CHUNKS = [list(range(TURNS - 3)), list(range(TURNS - 3, TURNS))]
LN_STEPS = 8
TWO_ONES = float(np.array([0x3F803F80], np.uint32).view(np.float32)[0])

assert KEYS % MAX_TURNS == 0 and MAX_KEYS <= 512
assert TILES % UNROLL == 0 and HEADS % 2 == 0 and 2 * HALVES * QG == 2 * NQ

def bank_uses(first, last, half):
    uses = [] if first else [("OT", half), ("Y", half)]
    if not last:
        uses += [("QP", half), ("QL", half)] + [("K", i) for i in KEY_CHUNKS[half]]
    return uses


def head_uses(first, last):
    return bank_uses(first, last, 0) + bank_uses(first, last, 1)


PRO_USES = [("QP", 0)] + [("K", i) for i in range(TURNS)] + [("QL", 0), ("QP", 1), ("QL", 1)]
TAIL_USES = [("OT", 0), ("Y", 0), ("OT", 1), ("Y", 1)]
BASE_0 = len(PRO_USES)
BASE_1 = BASE_0 + len(head_uses(True, False))
PER_HEAD = len(head_uses(False, False))
BASE_LAST = BASE_1 + (HEADS - 2) * PER_HEAD
BASE_TAIL = BASE_LAST + len(head_uses(False, True))


def build(nc, x, ctx_768, Wq, Wk, Wv, Wo, xbo, wf, uf, bf, wi, ui, bi, wc, uc, bc, wo, uo, fbo, in_c, out):
    stack = ExitStack()
    with stack:
        def sb(name, shape, dt):
            return stack.enter_context(nc.sbuf_tensor(name, shape, dt))

        def sem(name):
            return stack.enter_context(nc.semaphore(name))

        V = sb("V", [P, TILES * HEADS * VW], BF16)
        V4 = V[:, :].rearrange("p (t h c) -> p t h c", t=TILES, h=HEADS)
        K = sb("K", [P, 2 * KEYS], BF16)
        ctx_hi = sb("ctx_hi", [P, KEYS], BF16)
        ctx_lo = sb("ctx_lo", [P, KEYS], BF16)
        prob = sb("prob", [P, UNROLL, QG], F32)
        prob_lo = sb("prob_lo", [P, UNROLL, QG], BF16)
        qA = sb("qA", [P, 2, NQ], BF16)
        qB = sb("qB", [P, 2, NQ], BF16)
        q_low = sb("q_low", [P, QG], BF16)
        xnT_hi = sb("xnT_hi", [P, NQ], BF16)
        xnT_lo = sb("xnT_lo", [P, NQ], BF16)
        WqD_hi = sb("WqD_hi", [P, HEADS, 2, DH], BF16)
        WqD_lo = sb("WqD_lo", [P, HEADS, 2, DH], BF16)
        WkD_hi = sb("WkD_hi", [DC, HEADS, 2, DH], BF16)
        WkD_lo = sb("WkD_lo", [DC, HEADS, 2, DH], BF16)
        Wv_hi = sb("Wv_hi", [DC, HEADS * DH], BF16)
        Wv_lo = sb("Wv_lo", [DC, HEADS * DH], BF16)
        WkT = sb("WkT", [P, HEADS * DC], BF16)
        Wo_hi = sb("Wo_hi", [P, HEADS * DM], BF16)
        Wo_lo = sb("Wo_lo", [P, HEADS * DM], BF16)
        gateT = sb("gateT", [P, 5, P], F32)
        acc_raw = sb("acc_raw", [P, QT, VW], F32)
        o_norm = sb("o_norm", [P, QT, DH], F32)
        oT = sb("oT", [P, QG], BF16)
        yT = sb("yT", [P, NQ], F32)
        part_max = sb("part_max", [P, QT, MAX_TURNS], F32)
        neg_max = sb("neg_max", [P, QT], F32)
        neg_max2 = sb("neg_max2", [P, QT, 2], BF16)
        rden = sb("rden", [P, QT], F32)
        ident = sb("ident", [P, P], F32)
        identb = sb("identb", [P, P], BF16)
        stat = sb("stat", [P, 4, 8], F32)
        cols = sb("cols", [P, 8], F32)
        gate_bias = sb("gate_bias", [P, 3], F32)

        oT4 = oT[:, :].rearrange("p (k a q) -> p k a q", k=QT // 2, a=2)

        raw = V[:, :].bitcast(F32)
        ctx_raw = raw[:, 0:TILES * DC].rearrange("p (t c) -> p t c", t=TILES)
        nat_hi = V[:, 2 * TILES * DC:3 * TILES * DC]
        nat_lo = V[:, 3 * TILES * DC:4 * TILES * DC]
        at = 16000
        x_raw = raw[:, at:at + NQ].rearrange("p (n d) -> p n d", d=DM)
        x_sq = raw[:, at + 8 * NQ - 2048:at + 9 * NQ - 2048].rearrange("p (n d) -> p n d", d=DM)
        Wq_raw = raw[:, at + 1024:at + 1536]
        Wk_raw = raw[0:DC, at + 1536:at + 2048]
        Wv_raw = raw[0:DC, at + 2048:at + 2560]
        Wo_raw = raw[:, at + 2560:at + 3584]
        gate_raw = raw[:, at + 3584:at + 3584 + 8 * P].rearrange("p (w c) -> p w c", w=8)
        cbc = raw[:, at + 4608:at + 4608 + P]
        gsum = raw[:, at + 4736:at + 4736 + 3 * P].rearrange("p (w c) -> p w c", w=3)
        late = ctx_lo[:, :].bitcast(F32)
        x_late = late[:, 0:NQ].rearrange("p (n d) -> p n d", d=DM)
        x1 = late[:, NQ:2 * NQ].rearrange("p (n d) -> p n d", d=DM)
        xc = late[:, 2 * NQ:3 * NQ].rearrange("p (n d) -> p n d", d=DM)
        after = V[:, :].bitcast(F32)
        sq2 = after[:, 0:NQ].rearrange("p (n d) -> p n d", d=DM)
        xn2T = after[:, NQ:2 * NQ]
        fT = after[:, 2 * NQ:3 * NQ]
        iT = after[:, 3 * NQ:4 * NQ]
        gT = after[:, 4 * NQ:5 * NQ]
        cT = after[:, 5 * NQ:6 * NQ]
        hT = after[:, 6 * NQ:7 * NQ]
        res = after[:, 7 * NQ:8 * NQ].rearrange("p (n d) -> p n d", d=DM)

        sc = [stack.enter_context(nc.psum_tensor(f"sc{i}", [P, 512], F32)) for i in range(UNROLL)]
        mxb = [stack.enter_context(nc.psum_tensor(f"mxb{i}", [P, 512], F32)) for i in range(2)]
        acc = stack.enter_context(nc.psum_tensor("acc", [P, 2, 512], F32))
        bank = stack.enter_context(nc.psum_tensor("bank", [P, 512], F32))

        load_x = [sem(f"load_x{n}") for n in range(HALVES)]
        load_wk = sem("load_wk")
        load_wq = sem("load_wq")
        load_g = sem("load_g")
        load_wv = sem("load_wv")
        load_ctx = [sem(f"load_ctx{n}") for n in range(3)]
        load_late = sem("load_late")
        load_bias = sem("load_bias")
        stored = sem("stored")
        ident_ready = sem("ident_ready")
        power_ready = sem("power_ready")
        ones_ready = sem("ones_ready")
        ctx_ones = sem("ctx_ones")
        zeros_ready = sem("zeros_ready")
        w_hi = sem("w_hi")
        wsplit = sem("wsplit")
        nat_hi_done = sem("nat_hi_done")
        nat_lo_done = sem("nat_lo_done")
        pool_w = sem("pool_w")
        ln_step = sem("ln_step")
        ln_step2 = sem("ln_step2")
        xT_ready = sem("xT_ready")
        xT_hi = sem("xT_hi")
        xT_lo = sem("xT_lo")
        wT_ready = sem("wT_ready")
        wT_kept = sem("wT_kept")
        cT_hi_ready = sem("cT_hi_ready")
        cT_lo_ready = sem("cT_lo_ready")
        cT_hi = sem("cT_hi")
        cT_lo = sem("cT_lo")
        v_ready = sem("v_ready")
        v_hi = sem("v_hi")
        v_lo_dve = sem("v_lo_dve")
        v_kept = sem("v_kept")
        v_lo_pool = sem("v_lo_pool")
        gate_step = sem("gate_step")
        y_start = sem("y_start")

        bank_ready = sem("bank_ready")
        bank_hi = sem("bank_hi")
        bank_free = sem("bank_free")
        mx_ready = sem("mx_ready")
        rows_ready = sem("rows_ready")
        rows_kept = sem("rows_kept")
        mx_taken = sem("mx_taken")
        max_step = sem("max_step")
        sc_ready = sem("sc_ready")
        p_ready = sem("p_ready")
        lo_dve = sem("lo_dve")
        lo_pool = sem("lo_pool")
        pv_done = sem("pv_done")
        acc_taken = sem("acc_taken")
        fin_step = sem("fin_step")
        y_rows = sem("y_rows")
        x1_step = sem("x1_step")
        xn2_ready = sem("xn2_ready")
        xn2_kept = sem("xn2_kept")
        gate_ready = sem("gate_ready")
        gate_done = sem("gate_done")
        cell_step = sem("cell_step")
        o_ready = sem("o_ready")
        h_done = sem("h_done")
        h_rows = sem("h_rows")
        res_done = sem("res_done")

        def loop_pieces(last, half):
            return LOOP_LAST if last else LOOP_HALF_1 if half else LOOP_HALF_0

        def base(h, first, last):
            return BASE_0 if first else BASE_LAST if last else (h - 1) * PER_HEAD + BASE_1

        def use(h, first, last, half, what):
            at = (0 if half == 0 else len(bank_uses(first, last, 0))) + bank_uses(first, last, half).index(what)
            return base(h, first, last) + at

        def over_heads(eng, body):
            body(0, 0, True, False)
            with eng.Fori(0, (HEADS - 2) // 2) as pair:
                body(pair * 2 + 1, 1, False, False)
                body(pair * 2 + 2, 0, False, False)
            body(HEADS - 1, 1, False, True)

        block = stack.enter_context(nc.Block())

        @block.sync
        def _(sp):
            keys = ctx_768[0, 0:WHOLE * P].rearrange("(p t) c -> p t c", p=P)
            for n, n0, n1 in ((0, 0, QT), (1, QT, 2 * QT)):
                sp.dma_start(x_raw[:, n0:n1, :],
                             x[0].rearrange("(n p) d -> p n d", p=P)[:, n0:n1, :]).then_inc(load_x[n], 16)
                if n == 0:
                    sp.dma_start(Wk_raw, Wk).then_inc(load_wk, 16)
                    sp.dma_start(Wq_raw, Wq).then_inc(load_wq, 16)
            for n, (a, b) in enumerate(CTX_LOADS):
                if n > 0:
                    sp.dma_start(ctx_raw[:, a:b, :], keys[:, a:b, :]).then_inc(load_ctx[n], 16)
            sp.dma_start(ctx_raw[0:LAST, WHOLE, :], ctx_768[0, WHOLE * P:NKV]).then_inc(load_ctx[2], 16)
            sp.dma_start(ctx_raw[LAST:P, WHOLE, :], ctx_768[0, 0:P - LAST]).then_inc(load_ctx[2], 16)
            sp.dma_start(Wv_raw, Wv).then_inc(load_wv, 16)
            for a in range(2):
                sp.dma_start(Wo_raw[a * DH:(a + 1) * DH, :].rearrange("p (h c) -> p h c", h=HEADS),
                             Wo.rearrange("(h p) c -> p h c", p=DH)).then_inc(load_wv, 16)
            for n, w in enumerate([wf, wi, wc, uf, ui, uc, wo, uo]):
                sp.dma_start(gate_raw[:, n, :], w).then_inc(load_g, 16)
            for n, w in enumerate([bf, bi, bc]):
                sp.dma_start(cols[:, n:n + 1], w.rearrange("(p a) -> p a", a=1)).then_inc(load_g, 16)
            sp.dma_start(cols[:, 5:6], in_c.rearrange("(p a) -> p a", a=1)).then_inc(load_g, 16)
            sp.dma_start(cbc, in_c.rearrange("(a d) -> a d", a=1).broadcast_to([P, P])).then_inc(load_g, 16)
            sp.dma_start(cols[:, 3:4], fbo.rearrange("(p a) -> p a", a=1)).then_inc(load_bias, 16)
            sp.dma_start(cols[:, 4:5], xbo.rearrange("(p a) -> p a", a=1)).then_inc(load_bias, 16)
            sp.wait_ge(bank_free, use(HEADS - 2, False, False, 1, ("K", TURNS - 1)) + 1)
            sp.dma_start(x_late, x[0].rearrange("(n p) d -> p n d", p=P)).then_inc(load_late, 16)
            for half in range(HALVES):
                sp.wait_ge(res_done, half + 1)
                sp.dma_start(out[0].rearrange("(n p) d -> p n d", p=P)[:, half * QT:(half + 1) * QT, :],
                             res[:, half * QT:(half + 1) * QT, :]).then_inc(stored, 16)
            sp.wait_ge(stored, 16 * HALVES)

        @block.gpsimd
        def _(pool):
            def inverse_root(n0, n1, step, v):
                pool.wait_ge(step, v + 6)
                pool.wait_ge(power_ready, 1)
                pool.tensor_tensor(stat[:, 1, n0:n1], stat[:, 2, n0:n1], stat[:, 3, n0:n1],
                                   ALU.pow).then_inc(step, 1)

            pool.memset(stat[:, 3, :], -0.5).then_inc(power_ready, 1)
            pool.memset(ident[:, :], 0.0).then_inc(ident_ready, 1)
            pool.wait_ge(ident_ready, 1)
            nc.gpsimd.affine_select(out=ident[:, :], in_=ident[:, :], compare_op=ALU.not_equal, fill=1.0,
                                    base=0, pattern=[[-1, P]], channel_multiplier=1).then_inc(ident_ready, 1)
            pool.wait_ge(ident_ready, 2)
            pool.tensor_copy(identb[:, :], ident[:, :]).then_inc(ident_ready, 1)
            pool.wait_ge(ident_ready, 3)
            pool.memset(ctx_hi[DC:AUG, :].bitcast(F32), TWO_ONES).then_inc(ctx_ones, 1)
            pool.wait_ge(ctx_ones, 1)

            def context_low(g):
                a, b = g * CT * DC, min((g + 1) * CT, TILES) * DC
                pool.wait_ge(nat_hi_done, g + 1)
                pool.tensor_tensor(nat_lo[:, a:b], raw[:, a:b], nat_hi[:, a:b], ALU.subtract).then_inc(nat_lo_done, 1)

            context_low(0)
            inverse_root(0, QT, ln_step, 0)
            inverse_root(QT, 2 * QT, ln_step2, 0)
            for g in range(1, GROUPS):
                context_low(g)
            pool.wait_ge(w_hi, 4)
            pool.tensor_tensor(Wv_lo[:, :], Wv_raw, Wv_hi[:, :], ALU.subtract).then_inc(pool_w, 1)
            pool.tensor_tensor(Wo_lo[:, :], Wo_raw, Wo_hi[:, :], ALU.subtract).then_inc(pool_w, 1)

            pool.memset(yT[:, :], 0.0).then_inc(y_start, 1)
            pool.wait_ge(load_bias, 32)
            pool.wait_ge(y_start, 1)
            pool.tensor_scalar(yT[:, :], yT[:, :], cols[:, 4:5], None, ALU.add).then_inc(y_start, 1)

            def v_low(t, n, b, rows):
                pool.wait_ge(v_kept, n + 1)
                v = V[0:rows, ds(t * HEADS * VW, HEADS * VW)].rearrange("p (h c) -> p h c", h=HEADS)
                pool.tensor_tensor(v[:, :, DH + 1:VW], prob[0:rows, b, :].rearrange("p (h c) -> p h c", h=HEADS),
                                   v[:, :, 0:DH], ALU.subtract).then_inc(v_lo_pool, 1)

            pool.wait_ge(v_ready, 1)
            pool.memset(V4[:, 0:WHOLE, :, DH], 1.0).then_inc(ones_ready, 1)
            with pool.Fori(0, TURNS - 1) as i:
                v_low(i * UNROLL + 1, i * 2, 1, P)
                v_low(i * UNROLL + 2, i * 2 + 1, 2, P)
            v_low(TILES - 2, 2 * TURNS - 2, 1, P)
            pool.wait_ge(v_lo_pool, 2 * TURNS - 1)
            v_low(TILES - 1, 2 * TURNS - 1, 2, LAST)

            def low_part(n, j):
                pool.wait_ge(p_ready, n + 1)
                hi = prob[:, j, :].bitcast(BF16).rearrange("p (q two) -> p q two", two=2)[:, :, 1]
                pool.tensor_tensor(prob_lo[:, j, 0:POOL_COLS], prob[:, j, 0:POOL_COLS], hi[:, 0:POOL_COLS],
                                   ALU.subtract).then_inc(lo_pool, 1)

            with pool.Fori(0, HEADS * HALVES * TILES, UNROLL) as n:
                for j in range(UNROLL):
                    low_part(n + j, j)
            for half in range(HALVES):
                inverse_root(half * QT, (half + 1) * QT, x1_step, (1 + LN_STEPS) * half + 1)

        @block.tensor
        def _(pe):
            def take_bank(n):
                pe.wait_ge(bank_free, n)

            pe.wait_ge(ident_ready, 3)
            pe.wait_ge(load_wk, 16)
            for n in range(2):
                for k in range(4):
                    h = 4 * n + k
                    m = pe.transpose(sc[n][0:DH, k * DC:(k + 1) * DC], Wk_raw[:, h * DH:(h + 1) * DH],
                                     ident[0:DC, 0:DC])
                m.then_inc(wT_ready, 1)

            def x_turned(n):
                pe.wait_ge([ln_step, ln_step2][n], LN_STEPS)
                if n > 0:
                    pe.wait_ge(xT_lo, n)
                for k in range(QT):
                    m = pe.transpose(acc[:, 0, k * P:(k + 1) * P], x_raw[:, n * QT + k, :], ident[:, :])
                m.then_inc(xT_ready, 1)

            def context_turned(g):
                for nat, kept, taken, banks, ready in ((nat_hi, nat_hi_done, cT_hi, (mxb[0], sc[2]), cT_hi_ready),
                                                       (nat_lo, nat_lo_done, cT_lo, (mxb[1], acc[:, 1, :]),
                                                        cT_lo_ready)):
                    b = banks[g % 2][:, :] if g % 2 == 0 or banks[0] is mxb[0] else banks[1]
                    pe.wait_ge(kept, g + 1)
                    if g >= 2:
                        pe.wait_ge(taken, g - 1)
                    for j in range(min(CT, TILES - g * CT)):
                        off = (g * CT + j) * DC
                        m = pe.transpose(b.bitcast(BF16)[0:DC, j * P:(j + 1) * P], nat[:, off:off + DC],
                                         identb[:, :])
                    m.then_inc(ready, 1)

            def q_part(head, half, n):
                take_bank(n)
                s = slice(half * QG, (half + 1) * QG)
                whi = WqD_hi[:, :, :, :].rearrange("p h a d -> p (h a d)")[:, ds(head * P, P)]
                wlo = WqD_lo[:, :, :, :].rearrange("p h a d -> p (h a d)")[:, ds(head * P, P)]
                pe.matmul(bank[:, :], whi, xnT_hi[:, s], start=True, stop=False)
                pe.matmul(bank[:, :], wlo, xnT_hi[:, s], start=False, stop=False)
                pe.matmul(bank[:, :], whi, xnT_lo[:, s], start=False, stop=True).then_inc(bank_ready, 1)

            def q_low_part(head, n):
                take_bank(n)
                pe.matmul(bank[0:DC, :], WkT[:, ds(head * DC, DC)], q_low[:, :], start=True,
                          stop=True).then_inc(bank_ready, 1)

            def k_part(head, i, n):
                take_bank(n)
                whi = WkD_hi[:, :, :, :].rearrange("p h a d -> p (h a d)")[:, ds(head * P, P)]
                wlo = WkD_lo[:, :, :, :].rearrange("p h a d -> p (h a d)")[:, ds(head * P, P)]
                chi = ctx_hi[0:DC, ds(i * CHUNK, CHUNK)]
                clo = ctx_lo[0:DC, ds(i * CHUNK, CHUNK)]
                pe.matmul(bank[:, 0:CHUNK], whi, chi, start=True, stop=False)
                pe.matmul(bank[:, 0:CHUNK], wlo, chi, start=False, stop=False)
                pe.matmul(bank[:, 0:CHUNK], whi, clo, start=False, stop=True).then_inc(bank_ready, 1)

            def max_product(par, half, i, qt, m):
                if m is not None:
                    pe.wait_ge(mx_taken, m - 1)
                q = half * QG + qt * P
                pe.matmul(mxb[qt % 2][:, 0:MAX_KEYS], qA[:, par, q:q + P],
                          K[:, ds(par * KEYS + i * MAX_KEYS, MAX_KEYS)], start=True, stop=True).then_inc(mx_ready, 1)

            def minus_max_rows(g):
                pe.wait_ge(mx_taken, (g + 1) * MX)
                pe.wait_ge(max_step, g * 3 + 3)
                for qt in range(QT):
                    m = pe.transpose(mxb[1][:, :].bitcast(BF16)[0:2, qt * P:(qt + 1) * P], neg_max2[:, qt, :],
                                     identb[:, :])
                m.then_inc(rows_ready, 1)

            context_turned(0)
            x_turned(0)
            context_turned(1)
            pe.wait_ge(wsplit, 2)
            pe.wait_ge(xT_lo, 1)
            q_part(0, 0, 0)
            context_turned(2)
            k_part(0, 0, 1)
            context_turned(3)
            context_turned(4)
            x_turned(1)
            for g in range(5, GROUPS):
                context_turned(g)
            pe.wait_ge(load_g, 13 * 16)
            pe.wait_ge(wT_kept, 2)
            for n in range(5):
                b = sc[0] if n < 4 else sc[1]
                m = pe.transpose(b[:, (n % 4) * P:(n % 4 + 1) * P], gate_raw[:, [0, 1, 2, 6, 7][n], :], ident[:, :])
                if n >= 3:
                    m.then_inc(wT_ready, 1)
            pe.wait_ge(cT_hi, GROUPS)
            pe.wait_ge(cT_lo, GROUPS)
            pe.wait_ge(pool_w, 2)
            pe.wait_ge(wT_kept, 4)
            pe.wait_ge(gate_step, 4)

            def v_tile(i, j, first):
                if not first:
                    if j == 0:
                        pe.wait_ge(v_lo_dve, i)
                    else:
                        pe.wait_ge(v_kept, i * 2 + (j - 2))
                chi = ctx_hi[0:DC, ds((i * UNROLL + j) * P, P)]
                clo = ctx_lo[0:DC, ds((i * UNROLL + j) * P, P)]
                pe.matmul(sc[j][:, :], chi, Wv_hi[:, :], start=True, stop=False)
                pe.matmul(sc[j][:, :], chi, Wv_lo[:, :], start=False, stop=False)
                pe.matmul(sc[j][:, :], clo, Wv_hi[:, :], start=False, stop=True).then_inc(v_ready, 1)

            def v_turn(i, first, last):
                for j in range(UNROLL):
                    v_tile(i, j, first)
                    if j == 0:
                        if not first:
                            max_product(0, 0, i - 1, QT - 1, i * QT - 1)
                        pe.wait_ge(bank_free, i + 3)
                        if not last:
                            k_part(0, i + 2, i + 3)
                    max_product(0, 0, i, j, None if first and j < 2 else i * QT + j)

            k_part(0, 1, 2)
            v_turn(0, True, False)
            with pe.Fori(1, TURNS - 2) as i:
                v_turn(i, False, False)
            v_turn(TURNS - 2, False, True)
            v_tile(TURNS - 1, 0, False)
            max_product(0, 0, TURNS - 2, QT - 1, MX - 1)
            q_low_part(0, TURNS + 1)
            v_tile(TURNS - 1, 1, False)
            q_part(0, 1, TURNS + 2)
            minus_max_rows(0)
            v_tile(TURNS - 1, 2, False)

            def group_turn(h, par, half, first, last, i, kind, chunk=None):
                g = h * HALVES + half
                n0 = g * TILES + i * UNROLL
                npar, nhalf = (par, 1) if half == 0 else (1 - par, 0)
                start = first and half == 0 and kind == "open"
                q = slice(half * QG, (half + 1) * QG)

                def u(what):
                    return use(h, first, last, half, what)

                def maxima(qt):
                    max_product(npar, nhalf, i, qt, (g + 1) * MX + i * QT + qt)

                more = not (last and half == 1)
                with_maxima = kind != "last" and more

                def maxima_before():
                    if kind != "open" and more:
                        max_product(npar, nhalf, i - 1, QT - 1, (g + 1) * MX + (i - 1) * QT + QT - 1)

                def past_values(j):
                    hv, tv = h, (i - 1) * UNROLL + j
                    if kind == "open":
                        hv, tv = (h if half == 1 else h - 1), TILES - LAG + j
                    p_times_v(hv, tv, n0 + j - LAG, j, kind == "second" and j == 0, g)

                for j in range(UNROLL):
                    n = n0 + j
                    if not start:
                        pe.wait_ge(p_ready, n - 2)
                    if start and j == 0:
                        pe.wait_ge(v_lo_dve, TURNS)
                        pe.wait_ge(ctx_ones, 1)
                    if start and j > 0:
                        pe.wait_ge(v_kept, 2 * TURNS - 2 + j)
                    if first and half == 0 and kind == "second" and j == 0:
                        pe.wait_ge(v_lo_pool, 2 * TURNS)
                        pe.wait_ge(ones_ready, 3)
                    tile = ds(par * KEYS + (i * UNROLL + j) * P, P)
                    pe.matmul(sc[j][:, :], K[:, tile], qA[:, par, q], start=True, stop=False)
                    if kind == "open" and j == 0:
                        if not start:
                            past_values(0)
                        pe.wait_ge(rows_kept, g + 1)
                    pe.matmul(sc[j][:, :], ctx_hi[0:AUG, ds((i * UNROLL + j) * P, P)], qB[0:AUG, par, q],
                              start=False, stop=True).then_inc(sc_ready, 1)
                    if j == 0 and kind in ("second", "last"):
                        maxima_before()
                        if with_maxima:
                            maxima(0)
                    if not start and not (kind == "open" and j == 0):
                        past_values(j)
                    if kind == "last" and j == 2 and more:
                        minus_max_rows(g + 1)
                    if j == 0 and kind == "loop":
                        if chunk is None and half == 1 and more:
                            pe.wait_ge(bank_free, u(("K", TURNS - 1)) + 1)
                        maxima_before()
                    if j == 0 and kind in ("open", "loop") and with_maxima:
                        maxima(0)
                    if j == 0 and chunk is not None:
                        k_part(h + 1, i + (chunk - 2), u(("K", chunk)) + (i - 2))
                    if kind == "open" and j == 0 and not first:
                        turn_heads(g - 1, u(("OT", half)))
                    if kind == "second" and j == 0 and not last:
                        q_part(h + 1, half, u(("QP", half)))
                    if j == 1 and with_maxima:
                        maxima(1)
                    if start and j == 1:
                        q_low_part(0, TURNS + 3)
                    if kind == "open" and j == 2 and not first:
                        out_product(h - 1, u(("Y", half)))
                    if kind == "second" and j == 2 and not last:
                        q_low_part(h + 1, u(("QL", half)))
                    if j == 2 and with_maxima:
                        maxima(2)

            def p_times_v(hv, tv, n, slot, begin, g):
                pe.wait_ge(lo_dve, n + 1)
                pe.wait_ge(lo_pool, n + 1)
                if begin and not (isinstance(g, int) and g == 0):
                    pe.wait_ge(acc_taken, g)
                hi = prob[:, slot, :].bitcast(BF16).rearrange("p (q two) -> p q two", two=2)[:, :, 1]
                off = tv * (HEADS * VW) + hv * VW
                for qt in range(QT):
                    o = acc[:, qt // 2, (qt % 2) * VW:(qt % 2 + 1) * VW]
                    pe.matmul(o, hi[:, qt * P:(qt + 1) * P], V[:, ds(off, VW)], start=begin and qt % 2 == 0,
                              stop=False, skip_group_check=True)
                for qt in range(QT):
                    o = acc[:, qt // 2, (qt % 2) * VW:(qt % 2) * VW + DH + 1]
                    m = pe.matmul(o, prob_lo[:, slot, qt * P:(qt + 1) * P], V[:, ds(off, DH + 1)], start=False,
                                  stop=True, skip_group_check=True)
                m.then_inc(pv_done, 1)

            def turn_heads(g1, n):
                take_bank(n)
                pe.wait_ge(fin_step, g1 * 3)
                for k in range(QT // 2):
                    m = pe.transpose(bank[:, k * P:(k + 1) * P],
                                     o_norm[:, 2 * k:2 * k + 2, :].rearrange("p a d -> p (a d)"), ident[:, :])
                m.then_inc(bank_ready, 1)

            def out_product(head, n):
                take_bank(n)
                pe.matmul(bank[:, :], Wo_hi[:, ds(head * DM, DM)], oT[:, :], start=True, stop=False)
                pe.matmul(bank[:, :], Wo_lo[:, ds(head * DM, DM)], oT[:, :], start=False,
                          stop=True).then_inc(bank_ready, 1)

            def head_body(h, par, first, last):
                for half in range(HALVES):
                    group_turn(h, par, half, first, last, 0, "open")
                    group_turn(h, par, half, first, last, 1, "second")
                    for a, b, chunk in loop_pieces(last, half):
                        with pe.Fori(a, b) as i:
                            group_turn(h, par, half, first, last, i, "loop", chunk)
                    group_turn(h, par, half, first, last, TURNS - 1, "last")

            over_heads(pe, head_body)
            n_last = HEADS * HALVES * TILES
            turn_heads(HEADS * HALVES - 1, BASE_TAIL)
            for j in range(LAG):
                p_times_v(HEADS - 1, TILES - LAG + j, n_last - LAG + j, j, False, 1)
            out_product(HEADS - 1, BASE_TAIL + 1)
            turn_heads(HEADS * HALVES, BASE_TAIL + 2)
            out_product(HEADS - 1, BASE_TAIL + 3)

            for half in range(HALVES):
                pe.wait_ge(bank_free, BASE_TAIL + 2 + 2 * half)
                pe.wait_ge(p_ready, n_last)
                for k in range(QT):
                    c = (half * QT + k) * P
                    m = pe.transpose(sc[half][:, k * P:(k + 1) * P], yT[:, c:c + P], ident[:, :])
                m.then_inc(y_rows, 1)
            for half in range(HALVES):
                s = slice(half * QG, (half + 1) * QG)
                pe.wait_ge(x1_step, (1 + LN_STEPS) * (half + 1))
                for k in range(QT):
                    m = pe.transpose(mxb[half][:, k * P:(k + 1) * P], xc[:, half * QT + k, :], ident[:, :])
                m.then_inc(xn2_ready, 1)
                pe.wait_ge(xn2_kept, half + 1)
                for w, b in enumerate([sc[2][:, :], acc[:, 0, :], acc[:, 1, :]]):
                    if half == 0 and w == 1:
                        pe.wait_ge(acc_taken, HEADS * HALVES)
                    if half == 1:
                        pe.wait_ge(gate_done, w + 1)
                    pe.matmul(b, gateT[:, w, :], xn2T[:, s], start=True, stop=True).then_inc(gate_ready, 1)
            for half in range(HALVES):
                s = slice(half * QG, (half + 1) * QG)
                pe.matmul(sc[half][:, :], gateT[:, 3, :], xn2T[:, s], start=True, stop=False)
                pe.wait_ge(cell_step, 3 * (half + 1))
                pe.matmul(sc[half][:, :], gateT[:, 4, :], cT[:, s], start=False, stop=True).then_inc(o_ready, 1)
            for half in range(HALVES):
                pe.wait_ge(h_done, half + 1)
                for k in range(QT):
                    c = (half * QT + k) * P
                    m = pe.transpose(mxb[half][:, k * P:(k + 1) * P], hT[:, c:c + P], ident[:, :])
                m.then_inc(h_rows, 1)

        @block.scalar
        def _(act):
            keys = ctx_768[0, 0:WHOLE * P].rearrange("(p t) c -> p t c", p=P)
            a, b = CTX_LOADS[0]
            act.dma_start(ctx_raw[:, a:b, :], keys[:, a:b, :]).then_inc(load_ctx[0], 16)
            def context_split(g):
                a, b = g * CT, min((g + 1) * CT, TILES)
                n = min(g // 2, 2)
                act.wait_ge(load_ctx[n], 48 if n == 2 else 16)
                act.copy(nat_hi[:, a * DC:b * DC], raw[:, a * DC:b * DC]).then_inc(nat_hi_done, 1)

            def context_high(g):
                a, b = g * CT * P, min((g + 1) * CT, TILES) * P
                act.wait_ge(cT_hi_ready, g + 1)
                act.copy(ctx_hi[0:DC, a:b], [mxb[0], sc[2]][g % 2][:, :].bitcast(BF16)[0:DC, 0:b - a]
                         ).then_inc(cT_hi, 1)

            def x_high(n):
                act.wait_ge(xT_ready, n + 1)
                act.copy(xnT_hi[:, n * QG:(n + 1) * QG], acc[:, 0, :]).then_inc(xT_hi, 1)

            def q_high(par, half, n):
                act.wait_ge(bank_ready, n + 1)
                act.copy(qA[:, par, half * QG:(half + 1) * QG], bank[:, :]).then_inc(bank_hi, 1)

            def q_low_out(par, half, n):
                act.wait_ge(bank_ready, n + 1)
                act.copy(qB[0:DC, par, half * QG:(half + 1) * QG], bank[0:DC, :]).then_inc(bank_free, 1)

            def k_high(par, i, n):
                act.wait_ge(bank_ready, n + 1)
                act.copy(K[:, ds(par * KEYS + i * CHUNK, CHUNK)], bank[:, 0:CHUNK]).then_inc(bank_hi, 1)

            context_split(0)
            context_split(1)
            act.wait_ge(load_wk, 16)
            act.wait_ge(load_wq, 16)
            for w, hi in ((Wk_raw, WkD_hi), (Wq_raw, WqD_hi)):
                m = w.shape[0]
                act.copy(hi[0:m, :, :, :], w.rearrange("p (h a d) -> p h a d", h=HEADS, a=1)
                         .broadcast_to([m, HEADS, 2, DH])).then_inc(w_hi, 1)
            for n in range(2):
                act.wait_ge(wT_ready, n + 1)
                act.copy(WkT[0:DH, n * 4 * DC:(n + 1) * 4 * DC], sc[n][0:DH, 0:4 * DC]).then_inc(wT_kept, 1)
            context_high(0)
            x_high(0)
            context_split(2)
            context_high(1)
            context_split(3)
            context_split(4)
            q_high(0, 0, 0)
            context_high(2)
            context_split(5)
            k_high(0, 0, 1)
            context_split(6)
            act.wait_ge(load_wv, 48)
            act.copy(Wv_hi[:, :], Wv_raw).then_inc(w_hi, 1)
            context_high(3)
            context_high(4)
            act.copy(Wo_hi[:, :], Wo_raw).then_inc(w_hi, 1)
            x_high(1)
            for g in range(5, GROUPS):
                context_high(g)
            act.wait_ge(wT_ready, 3)
            act.copy(gateT[:, 0:4, :].rearrange("p a b -> p (a b)"), sc[0][:, :]).then_inc(wT_kept, 1)
            act.wait_ge(wT_ready, 4)
            act.copy(gateT[:, 4, :], sc[1][:, 0:P]).then_inc(wT_kept, 1)

            def v_high(t, n, b, rows):
                act.wait_ge(v_ready, t + 1)
                off = t * HEADS * VW
                dst = V[0:rows, ds(off, HEADS * VW)].rearrange("p (h c) -> p h c", h=HEADS)[:, :, 0:DH]
                act.copy(dst, sc[b][0:rows, :].rearrange("p (h c) -> p h c", h=HEADS)).then_inc(v_hi, 1)
                if b > 0:
                    if n is not None:
                        act.wait_ge(v_lo_pool, n)
                    act.copy(prob[0:rows, b, :], sc[b][0:rows, :]).then_inc(v_kept, 1)

            def v_turn(i, first, last):
                for j in range(UNROLL):
                    v_high(i * UNROLL + j, None if first else i * 2 + j - 2, j, P)
                    if j == 0 and not last:
                        k_high(0, i + 2, i + 3)

            k_high(0, 1, 2)
            v_turn(0, True, False)
            with act.Fori(1, TURNS - 2) as i:
                v_turn(i, False, False)
            v_turn(TURNS - 2, False, True)
            act.wait_ge(ones_ready, 2)
            v_high(TILES - 3, None, 0, P)
            q_low_out(0, 0, TURNS + 1)
            v_high(TILES - 2, 2 * TURNS - 3, 1, P)
            q_high(0, 1, TURNS + 2)

            def minus_max_rows(g, par, half):
                act.wait_ge(rows_ready, g + 1)
                act.copy(qB[DC:AUG, par, half * QG:(half + 1) * QG],
                         mxb[1][:, :].bitcast(BF16)[0:2, 0:QG]).then_inc(rows_kept, 1)

            def exp_tile(n, j, fresh):
                act.wait_ge(sc_ready, n + 1)
                if not fresh:
                    act.wait_ge(pv_done, n - 2)
                act.activation(prob[:, j, :], sc[j][:, :], ACT.Exp, scale=SCALE).then_inc(p_ready, 1)

            def group_turn(h, par, half, first, last, i, kind, chunk=None):
                g = h * HALVES + half
                n0 = g * TILES + i * UNROLL
                start = first and half == 0 and kind == "open"

                def u(what):
                    return use(h, first, last, half, what)

                for j in range(UNROLL):
                    if kind == "last" and j == 2 and not (last and half == 1):
                        minus_max_rows(g + 1, par if half == 0 else 1 - par, 1 - half)
                    if kind == "open" and j == 2 and not start:
                        take_sums(g, n0)
                    if start and j > 0:
                        act.wait_ge(v_lo_pool, 2 * TURNS - 2 + j)
                    exp_tile(n0 + j, j, start)
                    if start and j == 1:
                        q_low_out(0, 1, TURNS + 3)
                    if j == 0 and chunk is not None:
                        k_high(1 - par, i + (chunk - 2), u(("K", chunk)) + (i - 2))
                    if kind == "open" and j == 0 and not first:
                        heads_high(u(("OT", half)))
                    if kind == "second" and j == 0 and not last:
                        q_high(1 - par, half, u(("QP", half)))
                    if kind == "second" and j == 2 and not last:
                        q_low_out(1 - par, half, u(("QL", half)))

            def take_sums(g, n):
                act.wait_ge(pv_done, n)
                if not (isinstance(g, int) and g == 1):
                    act.wait_ge(fin_step, (g - 1) * 3)
                act.copy(acc_raw[:, :, :].rearrange("p (b t) c -> p b (t c)", b=2),
                         acc[:, :, 0:2 * VW]).then_inc(acc_taken, 1)

            def heads_high(n):
                act.wait_ge(bank_ready, n + 1)
                act.copy(oT4[0:DH, :, 0, :], bank[0:DH, 0:2 * P].rearrange("p (k q) -> p k q", k=2))
                act.copy(oT4[0:DH, :, 1, :], bank[DH:P, 0:2 * P].rearrange("p (k q) -> p k q", k=2)
                         ).then_inc(bank_hi, 1)

            def head_body(h, par, first, last):
                for half in range(HALVES):
                    group_turn(h, par, half, first, last, 0, "open")
                    group_turn(h, par, half, first, last, 1, "second")
                    for a, b, chunk in loop_pieces(last, half):
                        with act.Fori(a, b) as i:
                            group_turn(h, par, half, first, last, i, "loop", chunk)
                    group_turn(h, par, half, first, last, TURNS - 1, "last")

            minus_max_rows(0, 0, 0)
            v_high(TILES - 1, 2 * TURNS - 2, 2, LAST)
            over_heads(act, head_body)
            heads_high(BASE_TAIL)
            take_sums(HEADS * HALVES, HEADS * HALVES * TILES)
            heads_high(BASE_TAIL + 2)

            act.wait_ge(pv_done, HEADS * HALVES * TILES)
            act.wait_ge(gate_step, 5)
            for half in range(HALVES):
                s = slice(half * QG, (half + 1) * QG)
                act.wait_ge(xn2_ready, half + 1)
                act.copy(xn2T[:, s], mxb[half][:, :]).then_inc(xn2_kept, 1)
                for w, (dst, fn) in enumerate([(fT, ACT.Sigmoid), (iT, ACT.Sigmoid), (gT, ACT.Tanh)]):
                    act.wait_ge(gate_ready, 3 * half + w + 1)
                    b = sc[2][:, :] if w == 0 else acc[:, w - 1, :]
                    act.activation(dst[:, s], b, fn, bias=gate_bias[:, w:w + 1]).then_inc(gate_done, 1)
            for half in range(HALVES):
                s = slice(half * QG, (half + 1) * QG)
                act.wait_ge(o_ready, half + 1)
                act.activation(hT[:, s], sc[half][:, :], ACT.Tanh, bias=cols[:, 3:4]).then_inc(h_done, 1)

        @block.vector
        def _(dve):
            def layer_norm(src, dst, sq, n0, n1, sem_, v):
                n = n1 - n0
                mean, var = stat[:, 0, n0:n1], stat[:, 1, n0:n1]
                nrm = stat[:, 2, n0:n1]
                dve.tensor_reduce(mean, src[:, n0:n1, :], AX.X, ALU.add).then_inc(sem_, 1)
                dve.wait_ge(sem_, v + 1)
                dve.tensor_scalar(mean, mean, 1.0 / DM, None, ALU.mult).then_inc(sem_, 1)
                dve.wait_ge(sem_, v + 2)
                dve.tensor_tensor(dst[:, n0:n1, :], src[:, n0:n1, :],
                                  mean.rearrange("p (n a) -> p n a", a=1).broadcast_to([P, n, DM]),
                                  ALU.subtract).then_inc(sem_, 1)
                dve.wait_ge(sem_, v + 3)
                dve.tensor_tensor(sq[:, n0:n1, :], dst[:, n0:n1, :], dst[:, n0:n1, :], ALU.mult).then_inc(sem_, 1)
                dve.wait_ge(sem_, v + 4)
                dve.tensor_reduce(var, sq[:, n0:n1, :], AX.X, ALU.add).then_inc(sem_, 1)
                dve.wait_ge(sem_, v + 5)
                dve.tensor_scalar(nrm, var, 1.0 / DM, EPS, ALU.mult, ALU.add).then_inc(sem_, 1)

            def layer_norm_end(dst, n0, n1, sem_, v):
                n = n1 - n0
                var = stat[:, 1, n0:n1]
                dve.wait_ge(sem_, v + 6)
                dve.wait_ge(sem_, v + 7)
                dve.tensor_tensor(dst[:, n0:n1, :], dst[:, n0:n1, :],
                                  var.rearrange("p (n a) -> p n a", a=1).broadcast_to([P, n, DM]),
                                  ALU.mult).then_inc(sem_, 1)

            dve.memset(q_low[DH:P, :], 0.0).then_inc(zeros_ready, 1)
            dve.memset(WkT[DH:P, :], 0.0).then_inc(zeros_ready, 1)
            dve.memset(V4[:, WHOLE, :, :], 0.0).then_inc(ones_ready, 1)
            dve.wait_ge(ones_ready, 1)
            dve.memset(V4[0:LAST, WHOLE, :, DH], 1.0).then_inc(ones_ready, 1)

            def q_low_dve(par, half, nh):
                dve.wait_ge(bank_hi, nh)
                dve.tensor_tensor(q_low[0:DH, :], bank[0:DH, :], qA[0:DH, par, half * QG:(half + 1) * QG],
                                  ALU.subtract).then_inc(bank_free, 1)

            def k_low(par, i, nh):
                dve.wait_ge(bank_hi, nh)
                k = K[DH:P, ds(par * KEYS + i * CHUNK, CHUNK)]
                dve.tensor_tensor(k, bank[DH:P, 0:CHUNK], k, ALU.subtract).then_inc(bank_free, 1)

            def x_low(n):
                dve.wait_ge(xT_hi, n + 1)
                s = slice(n * QG, (n + 1) * QG)
                dve.tensor_tensor(xnT_lo[:, s], acc[:, 0, :], xnT_hi[:, s], ALU.subtract).then_inc(xT_lo, 1)

            def context_low(g):
                a, b = g * CT * P, min((g + 1) * CT, TILES) * P
                bank_g = mxb[1][:, :] if g % 2 == 0 else acc[:, 1, :]
                dve.wait_ge(cT_lo_ready, g + 1)
                dve.tensor_copy(ctx_lo[0:DC, a:b], bank_g.bitcast(BF16)[0:DC, 0:b - a]).then_inc(cT_lo, 1)

            dve.wait_ge(load_x[0], 16)
            layer_norm(x_raw, x_raw, x_sq, 0, QT, ln_step, 0)
            dve.wait_ge(load_x[1], 16)
            layer_norm(x_raw, x_raw, x_sq, QT, 2 * QT, ln_step2, 0)
            layer_norm_end(x_raw, 0, QT, ln_step, 0)
            for n, (w, hi, lo) in enumerate([(Wk_raw, WkD_hi, WkD_lo), (Wq_raw, WqD_hi, WqD_lo)]):
                m = w.shape[0]
                dve.wait_ge(w_hi, n + 1)
                dve.tensor_tensor(lo[0:m, :, :, :], w.rearrange("p (h a d) -> p h a d", h=HEADS, a=1)
                                  .broadcast_to([m, HEADS, 2, DH]), hi[0:m, :, :, :],
                                  ALU.subtract).then_inc(wsplit, 1)
            context_low(0)
            x_low(0)
            context_low(1)
            q_low_dve(0, 0, 1)
            context_low(2)
            k_low(0, 0, 2)
            context_low(3)
            layer_norm_end(x_raw, QT, 2 * QT, ln_step2, 0)
            context_low(4)
            x_low(1)
            for g in range(5, GROUPS):
                context_low(g)
            dve.wait_ge(load_g, 13 * 16)
            for w in range(3):
                dve.tensor_tensor(gsum[:, w, :], gate_raw[:, 3 + w, :], cbc, ALU.mult).then_inc(gate_step, 1)
            dve.wait_ge(gate_step, 3)
            dve.tensor_reduce(gate_bias[:, :], gsum, AX.X, ALU.add).then_inc(gate_step, 1)
            dve.wait_ge(gate_step, 4)
            dve.tensor_tensor(gate_bias[:, :], gate_bias[:, :], cols[:, 0:3], ALU.add).then_inc(gate_step, 1)
            def hand(uses, what, half=None):
                n = 0
                for k in uses:
                    if k[0] in ("QP", "K", "OT"):
                        n += 1
                    if k == what:
                        return n
                return n

            hb0 = 2 + TURNS
            hb1 = hb0 + hand(head_uses(True, False), None)
            per = hand(head_uses(False, False), None)
            hbl = hb1 + (HEADS - 2) * per
            hbt = hbl + hand(head_uses(False, True), None)

            def hands(h, first, last, half, what):
                b = hb0 if first else hbl if last else (h - 1) * per + hb1
                if half == 1:
                    b = b + hand(bank_uses(first, last, 0), None)
                return b + hand(bank_uses(first, last, half), what)

            def reduce_max(i, qt, m, fresh):
                if fresh is not None:
                    dve.wait_ge(max_step, fresh)
                dve.wait_ge(mx_ready, m + 1)
                dve.tensor_reduce(part_max[:, qt, ds(i, 1)], mxb[qt % 2][:, 0:MAX_KEYS], AX.X,
                                  ALU.max).then_inc(mx_taken, 1)

            def minus_max(g1):
                dve.wait_ge(mx_taken, g1 * MX)
                if not (isinstance(g1, int) and g1 == 1):
                    dve.wait_ge(max_step, (g1 - 1) * 3)
                dve.tensor_reduce(neg_max[:, :], part_max[:, :, :], AX.X, ALU.max, negate=True).then_inc(max_step, 1)
                dve.wait_ge(max_step, (g1 - 1) * 3 + 1)
                dve.tensor_copy(neg_max2[:, :, 0], neg_max[:, :]).then_inc(max_step, 1)
                dve.wait_ge(max_step, (g1 - 1) * 3 + 2)
                dve.tensor_tensor(neg_max2[:, :, 1], neg_max[:, :], neg_max2[:, :, 0],
                                  ALU.subtract).then_inc(max_step, 1)

            def v_low(t, b, rows):
                dve.wait_ge(v_hi, t + 1)
                v = V[0:rows, ds(t * HEADS * VW, HEADS * VW)].rearrange("p (h c) -> p h c", h=HEADS)
                dve.tensor_tensor(v[:, :, DH + 1:VW], sc[b][0:rows, :].rearrange("p (h c) -> p h c", h=HEADS),
                                  v[:, :, 0:DH], ALU.subtract).then_inc(v_lo_dve, 1)

            def v_turn(i, first, last):
                if not first:
                    reduce_max(i - 1, QT - 1, i * QT - 1, None)
                reduce_max(i, 0, i * QT, None)
                v_low(i * UNROLL, 0, P)
                reduce_max(i, 1, i * QT + 1, None)
                if not last:
                    k_low(0, i + 2, i + 4)
                reduce_max(i, 2, i * QT + 2, None)

            k_low(0, 1, 3)
            v_turn(0, True, False)
            with dve.Fori(1, TURNS - 2) as i:
                v_turn(i, False, False)
            v_turn(TURNS - 2, False, True)
            reduce_max(TURNS - 2, QT - 1, MX - 1, None)
            minus_max(1)
            v_low(TILES - UNROLL, 0, P)
            q_low_dve(0, 1, TURNS + 2)

            def low_part(n, j):
                dve.wait_ge(p_ready, n + 1)
                hi = prob[:, j, :].bitcast(BF16).rearrange("p (q two) -> p q two", two=2)[:, :, 1]
                dve.tensor_tensor(prob_lo[:, j, POOL_COLS:QG], prob[:, j, POOL_COLS:QG], hi[:, POOL_COLS:QG],
                                  ALU.subtract).then_inc(lo_dve, 1)

            def add_output(half, n):
                dve.wait_ge(bank_ready, n + 1)
                y = yT[:, half * QG:(half + 1) * QG]
                dve.tensor_tensor(y, bank[:, :], y, ALU.add).then_inc(bank_free, 1)

            def divide(g1):
                dve.wait_ge(acc_taken, g1)
                dve.reciprocal(rden[:, :], acc_raw[:, :, DH]).then_inc(fin_step, 1)
                dve.tensor_tensor(o_norm[:, :, :], acc_raw[:, :, 0:DH], acc_raw[:, :, DH + 1:VW],
                                  ALU.add).then_inc(fin_step, 1)
                dve.wait_ge(fin_step, (g1 - 1) * 3 + 2)
                dve.tensor_tensor(o_norm[:, :, :], o_norm[:, :, :],
                                  rden[:, :].rearrange("p (n a) -> p n a", a=1).broadcast_to([P, QT, DH]),
                                  ALU.mult).then_inc(fin_step, 1)

            def heads_low(nh):
                dve.wait_ge(bank_hi, nh)
                for a in range(2):
                    m = dve.tensor_tensor(oT4[DH:P, :, a, :],
                                          bank[a * DH:(a + 1) * DH, 0:2 * P].rearrange("p (k q) -> p k q", k=2),
                                          oT4[0:DH, :, a, :], ALU.subtract)
                m.then_inc(bank_free, 1)

            def group_turn(h, par, half, first, last, i, kind, chunk=None):
                g = h * HALVES + half
                n0 = g * TILES + i * UNROLL
                start = first and half == 0 and kind == "open"
                with_maxima = kind != "last" and not (last and half == 1)

                def maxima(qt):
                    if with_maxima:
                        reduce_max(i, qt, (g + 1) * MX + i * QT + qt, g * 3 + 1 if kind == "open" else None)

                if not start:
                    low_part(n0 - 1, UNROLL - 1)
                if kind != "open" and not (last and half == 1):
                    reduce_max(i - 1, QT - 1, (g + 1) * MX + (i - 1) * QT + QT - 1, None)
                if kind == "last" and not (last and half == 1):
                    minus_max(g + 2)
                maxima(0)
                low_part(n0, 0)
                if kind == "last" and not (first and half == 0):
                    divide(g)
                if kind == "open" and not first:
                    heads_low(hands(h, first, last, half, ("OT", half)))
                if kind == "second" and not last:
                    q_low_dve(1 - par, half, hands(h, first, last, half, ("QP", half)))
                if chunk is not None:
                    k_low(1 - par, i + (chunk - 2), hands(h, first, last, half, ("K", chunk)) + (i - 2))
                maxima(1)
                low_part(n0 + 1, 1)
                maxima(2)
                if kind == "open" and not first:
                    add_output(half, use(h, first, last, half, ("Y", half)))

            def head_body(h, par, first, last):
                for half in range(HALVES):
                    group_turn(h, par, half, first, last, 0, "open")
                    group_turn(h, par, half, first, last, 1, "second")
                    for a, b, chunk in loop_pieces(last, half):
                        with dve.Fori(a, b) as i:
                            group_turn(h, par, half, first, last, i, "loop", chunk)
                    group_turn(h, par, half, first, last, TURNS - 1, "last")

            dve.wait_ge(y_start, 2)
            over_heads(dve, head_body)
            n_last = HEADS * HALVES * TILES
            low_part(n_last - 1, (TILES - 1) % UNROLL)
            heads_low(hbt + 1)
            add_output(0, BASE_TAIL + 1)
            divide(HEADS * HALVES)
            heads_low(hbt + 2)
            add_output(1, BASE_TAIL + 3)

            dve.wait_ge(load_late, 16)
            dve.wait_ge(pv_done, n_last)
            for half in range(HALVES):
                a, b = half * QT, (half + 1) * QT
                dve.wait_ge(y_rows, half + 1)
                dve.tensor_tensor(x1[:, a:b, :], sc[half][:, :].rearrange("p (n d) -> p n d", d=DM),
                                  x_late[:, a:b, :], ALU.add).then_inc(x1_step, 1)
                dve.wait_ge(x1_step, (1 + LN_STEPS) * half + 1)
                layer_norm(x1, xc, sq2, a, b, x1_step, (1 + LN_STEPS) * half + 1)
                layer_norm_end(xc, a, b, x1_step, (1 + LN_STEPS) * half + 1)
            for half in range(HALVES):
                s = slice(half * QG, (half + 1) * QG)
                dve.wait_ge(gate_done, 3 * (half + 1))
                dve.tensor_scalar(fT[:, s], fT[:, s], cols[:, 5:6], None, ALU.mult).then_inc(cell_step, 1)
                dve.tensor_tensor(iT[:, s], iT[:, s], gT[:, s], ALU.mult).then_inc(cell_step, 1)
                dve.wait_ge(cell_step, 3 * half + 2)
                dve.tensor_tensor(cT[:, s], fT[:, s], iT[:, s], ALU.add).then_inc(cell_step, 1)
            for half in range(HALVES):
                a, b = half * QT, (half + 1) * QT
                dve.wait_ge(h_rows, half + 1)
                dve.tensor_tensor(res[:, a:b, :], mxb[half][:, :].rearrange("p (n d) -> p n d", d=DM),
                                  x1[:, a:b, :], ALU.add).then_inc(res_done, 1)


_INS = ["x", "ctx_768", "L0_xattn_Wq", "L0_xattn_Wk", "L0_xattn_Wv", "L0_xattn_Wo", "L0_xattn_bo",
        "L0_ffn_wf", "L0_ffn_uf", "L0_ffn_bf", "L0_ffn_wi", "L0_ffn_ui", "L0_ffn_bi",
        "L0_ffn_wc", "L0_ffn_uc", "L0_ffn_bc", "L0_ffn_wo", "L0_ffn_uo", "L0_ffn_bo", "L0_ffn_in_c"]


def kernel(**inputs):
    import numpy as _np
    import concourse.bacc as _bacc
    from concourse import mybir as _mybir
    from concourse.bass_utils import run_bass_kernel_spmd as _run

    nc = _bacc.Bacc("TRN2", target_bir_lowering=False, num_devices=1)
    arrays, args = {}, []
    for name in _INS:
        a = _np.ascontiguousarray(inputs[name])
        arrays[f"in_{name}_dram"] = a
        args.append(nc.dram_tensor(f"in_{name}_dram", a.shape, _mybir.dt.from_np(a.dtype), kind="ExternalInput").ap())
    out = nc.dram_tensor("out_0_dram", (1, NQ, DM), _mybir.dt.float32, kind="ExternalOutput").ap()
    build(nc, *args, out)
    r = _run(nc, [arrays], core_ids=[0])
    return r.results[0]["out_0_dram"]
```

```python
from contextlib import ExitStack

import numpy as np

import concourse.bass as bass
from concourse import mybir

F32 = mybir.dt.float32
BF16 = mybir.dt.bfloat16
ALU = mybir.AluOpType
ACT = mybir.ActivationFunctionType
AX = mybir.AxisListType
ds = bass.ds

P = 128
HEADS = 8
DH = 64
DM = 128
DC = 96
NQ = 1024
NKV = 6404
SCALE = DH ** -0.5
EPS = 1e-5

TILES = (NKV + P - 1) // P
WHOLE = NKV // P
LAST = NKV - WHOLE * P
UNROLL = 3
TURNS = TILES // UNROLL
CHUNK = UNROLL * P
QG = 512
QT = QG // P
HALVES = NQ // QG
VW = 2 * DH + 1
AUG = DC + 2
POOL_COLS = 320
POOL_COLS_FINAL = 224
KEYS = TILES * P
LAG = UNROLL
MAX_TURNS = TURNS - 1
MAX_KEYS = KEYS // MAX_TURNS
MX = MAX_TURNS * QT
CT = 8
GROUPS = -(-TILES // CT)
CTX_LOADS = [(0, 2 * CT), (2 * CT, 4 * CT), (4 * CT, WHOLE)]
LOOP_HALF_0 = [(2, TURNS - 1, 0)]
LOOP_HALF_1 = [(2, 5, TURNS - 3), (5, TURNS - 1, None)]
LOOP_LAST = [(2, TURNS - 1, None)]
(OT_TURN, OT_LOW_TURN, Y_TURN, Y_ADD_TURN, ROWS_TURN, SUM_TURN, MEAN_TURN, CENTRE_TURN, VAR_TURN, ROOT_TURN,
 NORM_TURN, TURNED_TURN, KEPT_TURN, LOW_TURN) = range(3, TURNS)
KEY_CHUNKS = [list(range(TURNS - 3)), list(range(TURNS - 3, TURNS))]
LN_STEPS = 8
TWO_ONES = float(np.array([0x3F803F80], np.uint32).view(np.float32)[0])

assert KEYS % MAX_TURNS == 0 and MAX_KEYS <= 512
assert TILES % UNROLL == 0 and HEADS % 2 == 0 and 2 * HALVES * QG == 2 * NQ

def bank_uses(first, last, half):
    uses = [] if first else [("OT", half), ("Y", half)]
    if not last:
        uses += [("QP", half), ("QL", half)] + [("K", i) for i in KEY_CHUNKS[half]]
    return uses


def head_uses(first, last):
    return bank_uses(first, last, 0) + bank_uses(first, last, 1)


PRO_USES = [("QP", 0)] + [("K", i) for i in range(TURNS)] + [("QL", 0), ("QP", 1), ("QL", 1)]
BASE_0 = len(PRO_USES)
BASE_1 = BASE_0 + len(head_uses(True, False))
PER_HEAD = len(head_uses(False, False))
BASE_LAST = BASE_1 + (HEADS - 2) * PER_HEAD
BASE_TAIL = BASE_LAST + len(head_uses(False, True))


def build(nc, x, ctx_768, Wq, Wk, Wv, Wo, xbo, wf, uf, bf, wi, ui, bi, wc, uc, bc, wo, uo, fbo, in_c, out):
    stack = ExitStack()
    with stack:
        def sb(name, shape, dt):
            return stack.enter_context(nc.sbuf_tensor(name, shape, dt))

        def sem(name):
            return stack.enter_context(nc.semaphore(name))

        V = sb("V", [P, TILES * HEADS * VW], BF16)
        V4 = V[:, :].rearrange("p (t h c) -> p t h c", t=TILES, h=HEADS)
        K = sb("K", [P, 2 * KEYS], BF16)
        ctx_hi = sb("ctx_hi", [P, KEYS], BF16)
        ctx_lo = sb("ctx_lo", [P, KEYS], BF16)
        prob = sb("prob", [P, UNROLL, QG], F32)
        prob_lo = sb("prob_lo", [P, UNROLL, QG], BF16)
        qA = sb("qA", [P, 2, NQ], BF16)
        qB = sb("qB", [P, 2, NQ], BF16)
        q_low = sb("q_low", [P, QG], BF16)
        xnT_hi = sb("xnT_hi", [P, NQ], BF16)
        xnT_lo = sb("xnT_lo", [P, NQ], BF16)
        WqD_hi = sb("WqD_hi", [P, HEADS, 2, DH], BF16)
        WqD_lo = sb("WqD_lo", [P, HEADS, 2, DH], BF16)
        WkD_hi = sb("WkD_hi", [DC, HEADS, 2, DH], BF16)
        WkD_lo = sb("WkD_lo", [DC, HEADS, 2, DH], BF16)
        Wv_hi = sb("Wv_hi", [DC, HEADS * DH], BF16)
        Wv_lo = sb("Wv_lo", [DC, HEADS * DH], BF16)
        WkT = sb("WkT", [P, HEADS * DC], BF16)
        Wo_hi = sb("Wo_hi", [P, HEADS * DM], BF16)
        Wo_lo = sb("Wo_lo", [P, HEADS * DM], BF16)
        gateT_hi = sb("gateT_hi", [P, 4, P], BF16)
        gateT_lo = sb("gateT_lo", [P, 4, P], BF16)
        uoT = sb("uoT", [P, P], F32)
        acc_raw = sb("acc_raw", [P, QT, VW], F32)
        o_norm = sb("o_norm", [P, QT, DH], F32)
        oT = sb("oT", [P, QG], BF16)
        yT = sb("yT", [P, NQ], F32)
        part_max = sb("part_max", [P, QT, MAX_TURNS], F32)
        neg_max = sb("neg_max", [P, QT], F32)
        neg_max2 = sb("neg_max2", [P, QT, 2], BF16)
        rden = sb("rden", [P, QT], F32)
        ident = sb("ident", [P, P], F32)
        identb = sb("identb", [P, P], BF16)
        stat = sb("stat", [P, 4, 8], F32)
        cols = sb("cols", [P, 8], F32)
        gate_bias = sb("gate_bias", [P, 3], F32)

        oT4 = oT[:, :].rearrange("p (k a q) -> p k a q", k=QT // 2, a=2)

        raw = V[:, :].bitcast(F32)
        ctx_raw = raw[:, 0:TILES * DC].rearrange("p (t c) -> p t c", t=TILES)
        nat_hi = V[:, 2 * TILES * DC:3 * TILES * DC]
        nat_lo = V[:, 3 * TILES * DC:4 * TILES * DC]
        at = 16000
        x_raw = raw[:, at:at + NQ].rearrange("p (n d) -> p n d", d=DM)
        x_sq = raw[:, at + 8 * NQ - 2048:at + 9 * NQ - 2048].rearrange("p (n d) -> p n d", d=DM)
        Wq_raw = raw[:, at + 1024:at + 1536]
        Wk_raw = raw[0:DC, at + 1536:at + 2048]
        Wv_raw = raw[0:DC, at + 2048:at + 2560]
        Wo_raw = raw[:, at + 2560:at + 3584]
        gate_raw = raw[:, at + 3584:at + 3584 + 8 * P].rearrange("p (w c) -> p w c", w=8)
        cbc = raw[:, at + 4608:at + 4608 + P]
        gsum = raw[:, at + 4736:at + 4736 + 3 * P].rearrange("p (w c) -> p w c", w=3)
        late = ctx_lo[:, :].bitcast(F32)
        x_late = late[:, 0:NQ].rearrange("p (n d) -> p n d", d=DM)
        x1 = late[:, NQ:2 * NQ].rearrange("p (n d) -> p n d", d=DM)
        xc = late[:, 2 * NQ:3 * NQ].rearrange("p (n d) -> p n d", d=DM)
        spare = K[:, 0:KEYS].bitcast(F32)
        after = V[:, :].bitcast(F32)
        xn2, fT, iT, gT, cT, hT = [[room[:, k * QG:(k + 1) * QG] for room in (spare, after)] for k in range(6)]
        xn2_hi, xn2_lo = [[room.bitcast(BF16)[:, a * QG:(a + 1) * QG] for room in xn2] for a in range(2)]
        sq2 = [room.rearrange("p (n d) -> p n d", d=DM)
               for room in (xnT_hi[:, :].bitcast(F32), after[:, 6 * QG:7 * QG])]
        res = [room.rearrange("p (n d) -> p n d", d=DM)
               for room in (xnT_lo[:, :].bitcast(F32), after[:, 7 * QG:8 * QG])]

        sc = [stack.enter_context(nc.psum_tensor(f"sc{i}", [P, 512], F32)) for i in range(UNROLL)]
        mxb = [stack.enter_context(nc.psum_tensor(f"mxb{i}", [P, 512], F32)) for i in range(2)]
        acc = stack.enter_context(nc.psum_tensor("acc", [P, 2, 512], F32))
        bank = stack.enter_context(nc.psum_tensor("bank", [P, 512], F32))

        load_x = [sem(f"load_x{n}") for n in range(HALVES)]
        load_wk = sem("load_wk")
        load_wq = sem("load_wq")
        load_g = sem("load_g")
        load_wv = sem("load_wv")
        load_ctx = [sem(f"load_ctx{n}") for n in range(3)]
        load_late = sem("load_late")
        load_bias = sem("load_bias")
        stored = sem("stored")
        ident_ready = sem("ident_ready")
        power_ready = sem("power_ready")
        ones_ready = sem("ones_ready")
        ctx_ones = sem("ctx_ones")
        zeros_ready = sem("zeros_ready")
        w_hi = sem("w_hi")
        wsplit = sem("wsplit")
        nat_hi_done = sem("nat_hi_done")
        nat_lo_done = sem("nat_lo_done")
        pool_w = sem("pool_w")
        ln_step = sem("ln_step")
        ln_step2 = sem("ln_step2")
        xT_ready = sem("xT_ready")
        xT_hi = sem("xT_hi")
        xT_lo = sem("xT_lo")
        wT_ready = sem("wT_ready")
        wT_kept = sem("wT_kept")
        cT_hi_ready = sem("cT_hi_ready")
        cT_lo_ready = sem("cT_lo_ready")
        cT_hi = sem("cT_hi")
        cT_lo = sem("cT_lo")
        v_ready = sem("v_ready")
        v_hi = sem("v_hi")
        v_lo_dve = sem("v_lo_dve")
        v_kept = sem("v_kept")
        v_lo_pool = sem("v_lo_pool")
        gate_step = sem("gate_step")
        gates_split = sem("gates_split")
        y_start = sem("y_start")

        bank_ready = sem("bank_ready")
        bank_hi = sem("bank_hi")
        bank_free = sem("bank_free")
        mx_ready = sem("mx_ready")
        rows_ready = sem("rows_ready")
        rows_kept = sem("rows_kept")
        mx_taken = sem("mx_taken")
        max_step = sem("max_step")
        sc_ready = sem("sc_ready")
        p_ready = sem("p_ready")
        lo_dve = sem("lo_dve")
        lo_pool = sem("lo_pool")
        pv_done = sem("pv_done")
        acc_taken = sem("acc_taken")
        fin_step = sem("fin_step")
        y_rows = sem("y_rows")
        x1_step = sem("x1_step")
        xn2_ready = sem("xn2_ready")
        xn2_kept = sem("xn2_kept")
        gate_ready = sem("gate_ready")
        gate_done = sem("gate_done")
        cell_step = sem("cell_step")
        o_ready = sem("o_ready")
        h_done = sem("h_done")
        h_rows = sem("h_rows")
        res_done = sem("res_done")

        def loop_pieces(last, half):
            return LOOP_LAST if last else LOOP_HALF_1 if half else LOOP_HALF_0

        def base(h, first, last):
            return BASE_0 if first else BASE_LAST if last else (h - 1) * PER_HEAD + BASE_1

        def use(h, first, last, half, what):
            at = (0 if half == 0 else len(bank_uses(first, last, 0))) + bank_uses(first, last, half).index(what)
            return base(h, first, last) + at

        def over_heads(eng, body):
            body(0, 0, True, False)
            with eng.Fori(0, (HEADS - 2) // 2) as pair:
                body(pair * 2 + 1, 1, False, False)
                body(pair * 2 + 2, 0, False, False)
            body(HEADS - 1, 1, False, True)

        block = stack.enter_context(nc.Block())

        @block.sync
        def _(sp):
            keys = ctx_768[0, 0:WHOLE * P].rearrange("(p t) c -> p t c", p=P)
            for n, n0, n1 in ((0, 0, QT), (1, QT, 2 * QT)):
                sp.dma_start(x_raw[:, n0:n1, :],
                             x[0].rearrange("(n p) d -> p n d", p=P)[:, n0:n1, :]).then_inc(load_x[n], 16)
                if n == 0:
                    sp.dma_start(Wk_raw, Wk).then_inc(load_wk, 16)
                    sp.dma_start(Wq_raw, Wq).then_inc(load_wq, 16)
            for n, (a, b) in enumerate(CTX_LOADS):
                if n > 0:
                    sp.dma_start(ctx_raw[:, a:b, :], keys[:, a:b, :]).then_inc(load_ctx[n], 16)
            sp.dma_start(ctx_raw[0:LAST, WHOLE, :], ctx_768[0, WHOLE * P:NKV]).then_inc(load_ctx[2], 16)
            sp.dma_start(ctx_raw[LAST:P, WHOLE, :], ctx_768[0, 0:P - LAST]).then_inc(load_ctx[2], 16)
            sp.dma_start(Wv_raw, Wv).then_inc(load_wv, 16)
            for a in range(2):
                sp.dma_start(Wo_raw[a * DH:(a + 1) * DH, :].rearrange("p (h c) -> p h c", h=HEADS),
                             Wo.rearrange("(h p) c -> p h c", p=DH)).then_inc(load_wv, 16)
            for n, w in enumerate([wf, wi, wc, uf, ui, uc, wo, uo]):
                sp.dma_start(gate_raw[:, n, :], w).then_inc(load_g, 16)
            for n, w in enumerate([bf, bi, bc]):
                sp.dma_start(cols[:, n:n + 1], w.rearrange("(p a) -> p a", a=1)).then_inc(load_g, 16)
            sp.dma_start(cols[:, 5:6], in_c.rearrange("(p a) -> p a", a=1)).then_inc(load_g, 16)
            sp.dma_start(cbc, in_c.rearrange("(a d) -> a d", a=1).broadcast_to([P, P])).then_inc(load_g, 16)
            sp.dma_start(cols[:, 3:4], fbo.rearrange("(p a) -> p a", a=1)).then_inc(load_bias, 16)
            sp.dma_start(cols[:, 4:5], xbo.rearrange("(p a) -> p a", a=1)).then_inc(load_bias, 16)
            sp.wait_ge(bank_free, use(HEADS - 2, False, False, 1, ("K", TURNS - 1)) + 1)
            sp.dma_start(x_late, x[0].rearrange("(n p) d -> p n d", p=P)).then_inc(load_late, 16)
            for half in range(HALVES):
                sp.wait_ge(res_done, half + 1)
                sp.dma_start(out[0].rearrange("(n p) d -> p n d", p=P)[:, half * QT:(half + 1) * QT, :],
                             res[half]).then_inc(stored, 16)
            sp.wait_ge(stored, 16 * HALVES)

        @block.gpsimd
        def _(pool):
            def inverse_root(n0, n1, step, v):
                pool.wait_ge(step, v + 6)
                pool.wait_ge(power_ready, 1)
                pool.tensor_tensor(stat[:, 1, n0:n1], stat[:, 2, n0:n1], stat[:, 3, n0:n1],
                                   ALU.pow).then_inc(step, 1)

            pool.memset(stat[:, 3, :], -0.5).then_inc(power_ready, 1)
            pool.memset(ident[:, :], 0.0).then_inc(ident_ready, 1)
            pool.wait_ge(ident_ready, 1)
            nc.gpsimd.affine_select(out=ident[:, :], in_=ident[:, :], compare_op=ALU.not_equal, fill=1.0,
                                    base=0, pattern=[[-1, P]], channel_multiplier=1).then_inc(ident_ready, 1)
            pool.wait_ge(ident_ready, 2)
            pool.tensor_copy(identb[:, :], ident[:, :]).then_inc(ident_ready, 1)
            pool.wait_ge(ident_ready, 3)
            pool.memset(ctx_hi[DC:AUG, :].bitcast(F32), TWO_ONES).then_inc(ctx_ones, 1)
            pool.wait_ge(ctx_ones, 1)

            pool.memset(yT[:, :], 0.0).then_inc(y_start, 1)

            def context_low(g):
                a, b = g * CT * DC, min((g + 1) * CT, TILES) * DC
                pool.wait_ge(nat_hi_done, g + 1)
                pool.tensor_tensor(nat_lo[:, a:b], raw[:, a:b], nat_hi[:, a:b], ALU.subtract).then_inc(nat_lo_done, 1)

            context_low(0)
            inverse_root(0, QT, ln_step, 0)
            inverse_root(QT, 2 * QT, ln_step2, 0)
            for g in range(1, GROUPS):
                context_low(g)
            pool.wait_ge(w_hi, 4)
            pool.tensor_tensor(Wv_lo[:, :], Wv_raw, Wv_hi[:, :], ALU.subtract).then_inc(pool_w, 1)
            pool.tensor_tensor(Wo_lo[:, :], Wo_raw, Wo_hi[:, :], ALU.subtract).then_inc(pool_w, 1)

            def v_low(t, n, b, rows):
                pool.wait_ge(v_kept, n + 1)
                v = V[0:rows, ds(t * HEADS * VW, HEADS * VW)].rearrange("p (h c) -> p h c", h=HEADS)
                pool.tensor_tensor(v[:, :, DH + 1:VW], prob[0:rows, b, :].rearrange("p (h c) -> p h c", h=HEADS),
                                   v[:, :, 0:DH], ALU.subtract).then_inc(v_lo_pool, 1)

            pool.wait_ge(v_ready, 2)
            pool.wait_ge(gate_step, 4)
            pool.wait_ge(pool_w, 2)
            pool.memset(V4[:, 0:WHOLE, :, DH], 1.0).then_inc(ones_ready, 1)
            with pool.Fori(0, TURNS - 1) as i:
                v_low(i * UNROLL + 1, i * 2, 1, P)
                v_low(i * UNROLL + 2, i * 2 + 1, 2, P)
            v_low(TILES - 2, 2 * TURNS - 2, 1, P)
            pool.wait_ge(v_lo_pool, 2 * TURNS - 1)
            v_low(TILES - 1, 2 * TURNS - 1, 2, LAST)

            def low_part(n, j, cols):
                pool.wait_ge(p_ready, n + 1)
                hi = prob[:, j, :].bitcast(BF16).rearrange("p (q two) -> p q two", two=2)[:, :, 1]
                pool.tensor_tensor(prob_lo[:, j, 0:cols], prob[:, j, 0:cols], hi[:, 0:cols],
                                   ALU.subtract).then_inc(lo_pool, 1)

            n_final = (HEADS * HALVES - 1) * TILES
            with pool.Fori(0, n_final, UNROLL) as n:
                for j in range(UNROLL):
                    low_part(n + j, j, POOL_COLS)
            cut = n_final + ROOT_TURN * UNROLL
            for a, b in ((n_final, cut), (cut, n_final + TILES)):
                with pool.Fori(a, b, UNROLL) as n:
                    for j in range(UNROLL):
                        low_part(n + j, j, POOL_COLS_FINAL)
                if b == cut:
                    inverse_root(0, QT, x1_step, 1)
            inverse_root(QT, 2 * QT, x1_step, LN_STEPS + 2)

        @block.tensor
        def _(pe):
            def take_bank(n):
                pe.wait_ge(bank_free, n)

            pe.wait_ge(ident_ready, 3)
            pe.wait_ge(load_wk, 16)
            for n in range(2):
                for k in range(4):
                    h = 4 * n + k
                    m = pe.transpose(sc[n][0:DH, k * DC:(k + 1) * DC], Wk_raw[:, h * DH:(h + 1) * DH],
                                     ident[0:DC, 0:DC])
                m.then_inc(wT_ready, 1)

            def x_turned(n):
                pe.wait_ge([ln_step, ln_step2][n], LN_STEPS)
                if n > 0:
                    pe.wait_ge(xT_lo, n)
                for k in range(QT):
                    m = pe.transpose(acc[:, 0, k * P:(k + 1) * P], x_raw[:, n * QT + k, :], ident[:, :])
                m.then_inc(xT_ready, 1)

            def context_turned(g):
                for nat, kept, taken, banks, ready in ((nat_hi, nat_hi_done, cT_hi, (mxb[0], sc[2]), cT_hi_ready),
                                                       (nat_lo, nat_lo_done, cT_lo, (mxb[1], acc[:, 1, :]),
                                                        cT_lo_ready)):
                    b = banks[g % 2][:, :]
                    pe.wait_ge(kept, g + 1)
                    if g >= 2:
                        pe.wait_ge(taken, g - 1)
                    for j in range(min(CT, TILES - g * CT)):
                        off = (g * CT + j) * DC
                        m = pe.transpose(b.bitcast(BF16)[0:DC, j * P:(j + 1) * P], nat[:, off:off + DC],
                                         identb[:, :])
                    m.then_inc(ready, 1)

            def q_part(head, half, n):
                take_bank(n)
                s = slice(half * QG, (half + 1) * QG)
                whi = WqD_hi[:, :, :, :].rearrange("p h a d -> p (h a d)")[:, ds(head * P, P)]
                wlo = WqD_lo[:, :, :, :].rearrange("p h a d -> p (h a d)")[:, ds(head * P, P)]
                pe.matmul(bank[:, :], whi, xnT_hi[:, s], start=True, stop=False)
                pe.matmul(bank[:, :], wlo, xnT_hi[:, s], start=False, stop=False)
                pe.matmul(bank[:, :], whi, xnT_lo[:, s], start=False, stop=True).then_inc(bank_ready, 1)

            def q_low_part(head, n):
                take_bank(n)
                pe.matmul(bank[0:DC, :], WkT[:, ds(head * DC, DC)], q_low[:, :], start=True,
                          stop=True).then_inc(bank_ready, 1)

            def k_part(head, i, n):
                take_bank(n)
                whi = WkD_hi[:, :, :, :].rearrange("p h a d -> p (h a d)")[:, ds(head * P, P)]
                wlo = WkD_lo[:, :, :, :].rearrange("p h a d -> p (h a d)")[:, ds(head * P, P)]
                chi = ctx_hi[0:DC, ds(i * CHUNK, CHUNK)]
                clo = ctx_lo[0:DC, ds(i * CHUNK, CHUNK)]
                pe.matmul(bank[:, 0:CHUNK], whi, chi, start=True, stop=False)
                pe.matmul(bank[:, 0:CHUNK], wlo, chi, start=False, stop=False)
                pe.matmul(bank[:, 0:CHUNK], whi, clo, start=False, stop=True).then_inc(bank_ready, 1)

            def max_product(par, half, i, qt, m):
                if m is not None:
                    pe.wait_ge(mx_taken, m - 1)
                q = half * QG + qt * P
                pe.matmul(mxb[qt % 2][:, 0:MAX_KEYS], qA[:, par, q:q + P],
                          K[:, ds(par * KEYS + i * MAX_KEYS, MAX_KEYS)], start=True, stop=True).then_inc(mx_ready, 1)

            def minus_max_rows(g):
                pe.wait_ge(mx_taken, (g + 1) * MX)
                pe.wait_ge(max_step, g * 3 + 3)
                for qt in range(QT):
                    m = pe.transpose(mxb[1][:, :].bitcast(BF16)[0:2, qt * P:(qt + 1) * P], neg_max2[:, qt, :],
                                     identb[:, :])
                m.then_inc(rows_ready, 1)

            context_turned(0)
            x_turned(0)
            context_turned(1)
            pe.wait_ge(wsplit, 2)
            pe.wait_ge(xT_lo, 1)
            q_part(0, 0, 0)
            context_turned(2)
            k_part(0, 0, 1)
            context_turned(3)
            context_turned(4)
            x_turned(1)
            pe.wait_ge(load_g, 13 * 16)
            pe.wait_ge(wT_kept, 2)
            for n in range(5):
                b = sc[0] if n < 4 else sc[1]
                m = pe.transpose(b[:, (n % 4) * P:(n % 4 + 1) * P], gate_raw[:, [0, 1, 2, 6, 7][n], :], ident[:, :])
                if n >= 3:
                    m.then_inc(wT_ready, 1)
            for g in range(5, GROUPS):
                context_turned(g)
            k_part(0, 1, 2)
            pe.wait_ge(pool_w, 1)
            pe.wait_ge(wT_kept, 4)
            pe.wait_ge(gates_split, 1)
            pe.wait_ge(cT_hi, GROUPS - 1)

            def v_tile(i, j, first):
                if not first:
                    if j == 0:
                        pe.wait_ge(v_lo_dve, i)
                    else:
                        pe.wait_ge(v_kept, i * 2 + (j - 2))
                chi = ctx_hi[0:DC, ds((i * UNROLL + j) * P, P)]
                clo = ctx_lo[0:DC, ds((i * UNROLL + j) * P, P)]
                pe.matmul(sc[j][:, :], chi, Wv_hi[:, :], start=True, stop=False)
                pe.matmul(sc[j][:, :], chi, Wv_lo[:, :], start=False, stop=False)
                pe.matmul(sc[j][:, :], clo, Wv_hi[:, :], start=False, stop=True).then_inc(v_ready, 1)

            def v_turn(i, first, last):
                for j in range(UNROLL):
                    v_tile(i, j, first)
                    if j == 0 and first:
                        pe.wait_ge(cT_hi, GROUPS)
                        pe.wait_ge(cT_lo, GROUPS)
                    if j == 0:
                        if not first:
                            max_product(0, 0, i - 1, QT - 1, i * QT - 1)
                        pe.wait_ge(bank_free, i + 3)
                        if not last:
                            k_part(0, i + 2, i + 3)
                    max_product(0, 0, i, j, None if first and j < 2 else i * QT + j)

            v_turn(0, True, False)
            with pe.Fori(1, TURNS - 2) as i:
                v_turn(i, False, False)
            v_turn(TURNS - 2, False, True)
            v_tile(TURNS - 1, 0, False)
            max_product(0, 0, TURNS - 2, QT - 1, MX - 1)
            q_low_part(0, TURNS + 1)
            v_tile(TURNS - 1, 1, False)
            q_part(0, 1, TURNS + 2)
            minus_max_rows(0)
            v_tile(TURNS - 1, 2, False)

            def group_turn(h, par, half, first, last, i, kind, chunk=None):
                g = h * HALVES + half
                n0 = g * TILES + i * UNROLL
                npar, nhalf = (par, 1) if half == 0 else (1 - par, 0)
                start = first and half == 0 and kind == "open"
                q = slice(half * QG, (half + 1) * QG)

                def u(what):
                    return use(h, first, last, half, what)

                def maxima(qt):
                    max_product(npar, nhalf, i, qt, (g + 1) * MX + i * QT + qt)

                more = not (last and half == 1)
                with_maxima = kind != "last" and more

                def maxima_before():
                    if kind != "open" and more:
                        max_product(npar, nhalf, i - 1, QT - 1, (g + 1) * MX + (i - 1) * QT + QT - 1)

                def past_values(j):
                    hv, tv = h, (i - 1) * UNROLL + j
                    if kind == "open":
                        hv, tv = (h if half == 1 else h - 1), TILES - LAG + j
                    p_times_v(hv, tv, n0 + j - LAG, j, kind == "second" and j == 0, g)

                for j in range(UNROLL):
                    n = n0 + j
                    if not start:
                        pe.wait_ge(p_ready, n - 2)
                    if start and j == 0:
                        pe.wait_ge(v_lo_dve, TURNS)
                        pe.wait_ge(ctx_ones, 1)
                    if start and j > 0:
                        pe.wait_ge(v_kept, 2 * TURNS - 2 + j)
                    if first and half == 0 and kind == "second" and j == 0:
                        pe.wait_ge(v_lo_pool, 2 * TURNS)
                        pe.wait_ge(ones_ready, 3)
                        pe.wait_ge(pool_w, 2)
                    tile = ds(par * KEYS + (i * UNROLL + j) * P, P)
                    pe.matmul(sc[j][:, :], K[:, tile], qA[:, par, q], start=True, stop=False)
                    if j == 1 and with_maxima and kind == "loop" and chunk is None:
                        maxima(0)
                    if kind == "open" and j == 0:
                        if not start:
                            past_values(0)
                        pe.wait_ge(rows_kept, g + 1)
                    pe.matmul(sc[j][:, :], ctx_hi[0:AUG, ds((i * UNROLL + j) * P, P)], qB[0:AUG, par, q],
                              start=False, stop=True).then_inc(sc_ready, 1)
                    if j == 0 and kind in ("second", "last"):
                        maxima_before()
                        if with_maxima:
                            maxima(0)
                    if not start and not (kind == "open" and j == 0):
                        past_values(j)
                    if kind == "last" and j == 2 and more:
                        minus_max_rows(g + 1)
                    if j == 0 and kind == "loop":
                        if chunk is None and half == 1 and more:
                            pe.wait_ge(bank_free, u(("K", TURNS - 1)) + 1)
                        maxima_before()
                    if j == 0 and chunk is not None:
                        k_part(h + 1, i + (chunk - 2), u(("K", chunk)) + (i - 2))
                    if j == 0 and with_maxima and (kind == "open" or chunk is not None):
                        maxima(0)
                    if kind == "open" and j == 0 and not first:
                        turn_heads(g - 1, u(("OT", half)))
                    if kind == "second" and j == 0 and not last:
                        q_part(h + 1, half, u(("QP", half)))
                    if j == 1 and with_maxima:
                        maxima(1)
                    if start and j == 1:
                        q_low_part(0, TURNS + 3)
                    if kind == "open" and j == 2 and not first:
                        out_product(h - 1, u(("Y", half)))
                    if kind == "second" and j == 2 and not last:
                        q_low_part(h + 1, u(("QL", half)))
                    if j == 2 and with_maxima:
                        maxima(2)

            def p_times_v(hv, tv, n, slot, begin, g):
                pe.wait_ge(lo_dve, n + 1)
                pe.wait_ge(lo_pool, n + 1)
                if begin and not (isinstance(g, int) and g == 0):
                    pe.wait_ge(acc_taken, g)
                hi = prob[:, slot, :].bitcast(BF16).rearrange("p (q two) -> p q two", two=2)[:, :, 1]
                off = tv * (HEADS * VW) + hv * VW
                for qt in range(QT):
                    o = acc[:, qt // 2, (qt % 2) * VW:(qt % 2 + 1) * VW]
                    pe.matmul(o, hi[:, qt * P:(qt + 1) * P], V[:, ds(off, VW)], start=begin and qt % 2 == 0,
                              stop=False, skip_group_check=True)
                for qt in range(QT):
                    o = acc[:, qt // 2, (qt % 2) * VW:(qt % 2) * VW + DH + 1]
                    m = pe.matmul(o, prob_lo[:, slot, qt * P:(qt + 1) * P], V[:, ds(off, DH + 1)], start=False,
                                  stop=True, skip_group_check=True)
                m.then_inc(pv_done, 1)

            def turn_heads(g1, n):
                take_bank(n)
                pe.wait_ge(fin_step, g1 * 3)
                for k in range(QT // 2):
                    m = pe.transpose(bank[:, k * P:(k + 1) * P],
                                     o_norm[:, 2 * k:2 * k + 2, :].rearrange("p a d -> p (a d)"), ident[:, :])
                m.then_inc(bank_ready, 1)

            def out_product(head, n):
                take_bank(n)
                pe.matmul(bank[:, :], Wo_hi[:, ds(head * DM, DM)], oT[:, :], start=True, stop=False)
                pe.matmul(bank[:, :], Wo_lo[:, ds(head * DM, DM)], oT[:, :], start=False,
                          stop=True).then_inc(bank_ready, 1)

            def head_body(h, par, first, last):
                for half in range(HALVES):
                    group_turn(h, par, half, first, last, 0, "open")
                    group_turn(h, par, half, first, last, 1, "second")
                    if last and half == 1:
                        for i in range(2, TURNS - 1):
                            half_0_step(i)
                            group_turn(h, par, half, first, last, i, "loop")
                    else:
                        for a, b, chunk in loop_pieces(last, half):
                            with pe.Fori(a, b) as i:
                                group_turn(h, par, half, first, last, i, "loop", chunk)
                    if last and half == 1:
                        half_0_step(TURNS - 1)
                    group_turn(h, par, half, first, last, TURNS - 1, "last")

            def output_rows(half, b):
                pe.wait_ge(bank_free, BASE_TAIL + 2 + 2 * half)
                for k in range(QT):
                    c = (half * QT + k) * P
                    m = pe.transpose(b[:, k * P:(k + 1) * P], yT[:, c:c + P], ident[:, :])
                m.then_inc(y_rows, 1)

            def normalised_turned(half, b):
                pe.wait_ge(x1_step, (1 + LN_STEPS) * (half + 1))
                for k in range(QT):
                    m = pe.transpose(b[:, k * P:(k + 1) * P], xc[:, half * QT + k, :], ident[:, :])
                m.then_inc(xn2_ready, 1)

            def times_normalised(half, w, b, stop):
                pe.matmul(b, gateT_hi[:, w, :], xn2_hi[half], start=True, stop=False)
                pe.matmul(b, gateT_lo[:, w, :], xn2_hi[half], start=False, stop=False)
                return pe.matmul(b, gateT_hi[:, w, :], xn2_lo[half], start=False, stop=stop)

            def gate(half, w, b):
                times_normalised(half, w, b, True).then_inc(gate_ready, 1)

            def half_0_step(turn):
                if turn == OT_TURN:
                    turn_heads(HEADS * HALVES - 1, BASE_TAIL)
                elif turn == Y_TURN:
                    out_product(HEADS - 1, BASE_TAIL + 1)
                elif turn == ROWS_TURN:
                    output_rows(0, mxb[0])
                elif turn == TURNED_TURN:
                    normalised_turned(0, mxb[1])

            over_heads(pe, head_body)
            n_last = HEADS * HALVES * TILES
            for j in range(LAG):
                p_times_v(HEADS - 1, TILES - LAG + j, n_last - LAG + j, j, False, 1)
            pe.wait_ge(xn2_kept, 2)
            pe.wait_ge(x1_step, 1)
            gate(0, 0, mxb[0][:, :])
            gate(0, 1, mxb[1][:, :])
            pe.wait_ge(p_ready, n_last)
            gate(0, 2, sc[0][:, :])
            turn_heads(HEADS * HALVES, BASE_TAIL + 2)
            out_product(HEADS - 1, BASE_TAIL + 3)
            output_rows(1, sc[1])

            def gate_o_state(half, b):
                pe.wait_ge(cell_step, 3 * (half + 1))
                pe.matmul(b, uoT[:, :], cT[half], start=False, stop=True).then_inc(o_ready, 1)

            def hidden_rows(half, b):
                pe.wait_ge(h_done, half + 1)
                for k in range(QT):
                    m = pe.transpose(b[:, k * P:(k + 1) * P], hT[half][:, k * P:(k + 1) * P], ident[:, :])
                m.then_inc(h_rows, 1)

            pe.wait_ge(gate_done, 3)
            times_normalised(0, 3, mxb[1][:, :], False)
            normalised_turned(1, sc[2])
            gate_o_state(0, mxb[1][:, :])
            pe.wait_ge(xn2_kept, 4)
            pe.wait_ge(acc_taken, HEADS * HALVES)
            gate(1, 0, acc[:, 0, :])
            gate(1, 1, acc[:, 1, :])
            gate(1, 2, mxb[0][:, :])
            times_normalised(1, 3, sc[1][:, :], False)
            hidden_rows(0, sc[0])
            gate_o_state(1, sc[1][:, :])
            hidden_rows(1, sc[2])

        @block.scalar
        def _(act):
            keys = ctx_768[0, 0:WHOLE * P].rearrange("(p t) c -> p t c", p=P)
            a, b = CTX_LOADS[0]
            act.dma_start(ctx_raw[:, a:b, :], keys[:, a:b, :]).then_inc(load_ctx[0], 16)
            def context_split(g):
                a, b = g * CT, min((g + 1) * CT, TILES)
                n = min(g // 2, 2)
                act.wait_ge(load_ctx[n], 48 if n == 2 else 16)
                act.copy(nat_hi[:, a * DC:b * DC], raw[:, a * DC:b * DC]).then_inc(nat_hi_done, 1)

            def context_high(g):
                a, b = g * CT * P, min((g + 1) * CT, TILES) * P
                act.wait_ge(cT_hi_ready, g + 1)
                act.copy(ctx_hi[0:DC, a:b], [mxb[0], sc[2]][g % 2][:, :].bitcast(BF16)[0:DC, 0:b - a]
                         ).then_inc(cT_hi, 1)

            def x_high(n):
                act.wait_ge(xT_ready, n + 1)
                act.copy(xnT_hi[:, n * QG:(n + 1) * QG], acc[:, 0, :]).then_inc(xT_hi, 1)

            def q_high(par, half, n):
                act.wait_ge(bank_ready, n + 1)
                act.copy(qA[:, par, half * QG:(half + 1) * QG], bank[:, :]).then_inc(bank_hi, 1)

            def q_low_out(par, half, n):
                act.wait_ge(bank_ready, n + 1)
                act.copy(qB[0:DC, par, half * QG:(half + 1) * QG], bank[0:DC, :]).then_inc(bank_free, 1)

            def k_high(par, i, n):
                act.wait_ge(bank_ready, n + 1)
                act.copy(K[:, ds(par * KEYS + i * CHUNK, CHUNK)], bank[:, 0:CHUNK]).then_inc(bank_hi, 1)

            context_split(0)
            context_split(1)
            act.wait_ge(load_wk, 16)
            act.wait_ge(load_wq, 16)
            for w, hi in ((Wk_raw, WkD_hi), (Wq_raw, WqD_hi)):
                m = w.shape[0]
                act.copy(hi[0:m, :, :, :], w.rearrange("p (h a d) -> p h a d", h=HEADS, a=1)
                         .broadcast_to([m, HEADS, 2, DH])).then_inc(w_hi, 1)
            for n in range(2):
                act.wait_ge(wT_ready, n + 1)
                act.copy(WkT[0:DH, n * 4 * DC:(n + 1) * 4 * DC], sc[n][0:DH, 0:4 * DC]).then_inc(wT_kept, 1)
            context_high(0)
            x_high(0)
            context_split(2)
            context_high(1)
            context_split(3)
            context_split(4)
            q_high(0, 0, 0)
            context_high(2)
            context_split(5)
            k_high(0, 0, 1)
            context_split(6)
            act.wait_ge(load_wv, 48)
            act.copy(Wv_hi[:, :], Wv_raw).then_inc(w_hi, 1)
            context_high(3)
            context_high(4)
            act.copy(Wo_hi[:, :], Wo_raw).then_inc(w_hi, 1)
            x_high(1)
            act.wait_ge(wT_ready, 3)
            act.copy(gateT_hi[:, :, :].rearrange("p a b -> p (a b)"), sc[0][:, :]).then_inc(wT_kept, 1)
            act.wait_ge(wT_ready, 4)
            act.copy(uoT[:, :], sc[1][:, 0:P]).then_inc(wT_kept, 1)
            for g in range(5, GROUPS):
                context_high(g)
            def v_high(t, n, b, rows):
                act.wait_ge(v_ready, t + 1)
                off = t * HEADS * VW
                dst = V[0:rows, ds(off, HEADS * VW)].rearrange("p (h c) -> p h c", h=HEADS)[:, :, 0:DH]
                act.copy(dst, sc[b][0:rows, :].rearrange("p (h c) -> p h c", h=HEADS)).then_inc(v_hi, 1)
                if b > 0:
                    if n is not None:
                        act.wait_ge(v_lo_pool, n)
                    act.copy(prob[0:rows, b, :], sc[b][0:rows, :]).then_inc(v_kept, 1)

            def v_turn(i, first, last):
                for j in range(UNROLL):
                    v_high(i * UNROLL + j, None if first else i * 2 + j - 2, j, P)
                    if j == 0 and not last:
                        k_high(0, i + 2, i + 3)

            k_high(0, 1, 2)
            v_turn(0, True, False)
            with act.Fori(1, TURNS - 2) as i:
                v_turn(i, False, False)
            v_turn(TURNS - 2, False, True)
            act.wait_ge(ones_ready, 2)
            v_high(TILES - 3, None, 0, P)
            q_low_out(0, 0, TURNS + 1)
            v_high(TILES - 2, 2 * TURNS - 3, 1, P)
            q_high(0, 1, TURNS + 2)

            def minus_max_rows(g, par, half):
                act.wait_ge(rows_ready, g + 1)
                act.copy(qB[DC:AUG, par, half * QG:(half + 1) * QG],
                         mxb[1][:, :].bitcast(BF16)[0:2, 0:QG]).then_inc(rows_kept, 1)

            def exp_tile(n, j, fresh):
                act.wait_ge(sc_ready, n + 1)
                if not fresh:
                    act.wait_ge(pv_done, n - 2)
                act.activation(prob[:, j, :], sc[j][:, :], ACT.Exp, scale=SCALE).then_inc(p_ready, 1)

            def group_turn(h, par, half, first, last, i, kind, chunk=None):
                g = h * HALVES + half
                n0 = g * TILES + i * UNROLL
                start = first and half == 0 and kind == "open"

                def u(what):
                    return use(h, first, last, half, what)

                for j in range(UNROLL):
                    if kind == "last" and j == 2 and not (last and half == 1):
                        minus_max_rows(g + 1, par if half == 0 else 1 - par, 1 - half)
                    if kind == "open" and j == 2 and not start:
                        take_sums(g, n0)
                    if start and j > 0:
                        act.wait_ge(v_lo_pool, 2 * TURNS - 2 + j)
                    exp_tile(n0 + j, j, start)
                    if start and j == 1:
                        q_low_out(0, 1, TURNS + 3)
                    if j == 0 and chunk is not None:
                        k_high(1 - par, i + (chunk - 2), u(("K", chunk)) + (i - 2))
                    if kind == "open" and j == 0 and not first:
                        heads_high(u(("OT", half)))
                    if kind == "second" and j == 0 and not last:
                        q_high(1 - par, half, u(("QP", half)))
                    if kind == "second" and j == 2 and not last:
                        q_low_out(1 - par, half, u(("QL", half)))

            def take_sums(g, n):
                act.wait_ge(pv_done, n)
                if not (isinstance(g, int) and g == 1):
                    act.wait_ge(fin_step, (g - 1) * 3)
                act.copy(acc_raw[:, :, :].rearrange("p (b t) c -> p b (t c)", b=2),
                         acc[:, :, 0:2 * VW]).then_inc(acc_taken, 1)

            def heads_high(n):
                act.wait_ge(bank_ready, n + 1)
                act.copy(oT4[0:DH, :, 0, :], bank[0:DH, 0:2 * P].rearrange("p (k q) -> p k q", k=2))
                act.copy(oT4[0:DH, :, 1, :], bank[DH:P, 0:2 * P].rearrange("p (k q) -> p k q", k=2)
                         ).then_inc(bank_hi, 1)

            def half_0_step(turn):
                if turn == OT_TURN:
                    heads_high(BASE_TAIL)
                elif turn == KEPT_TURN:
                    normalised(0, mxb[1])

            def normalised(half, b):
                act.wait_ge(xn2_ready, half + 1)
                act.copy(xn2_hi[half], b[:, :]).then_inc(xn2_kept, 1)

            def gate(half, w, b):
                act.wait_ge(gate_ready, 3 * half + w + 1)
                act.activation((fT, iT, gT)[w][half], b, (ACT.Sigmoid, ACT.Sigmoid, ACT.Tanh)[w],
                               bias=gate_bias[:, w:w + 1]).then_inc(gate_done, 1)

            def hidden(half, b):
                act.wait_ge(o_ready, half + 1)
                act.activation(hT[half], b, ACT.Tanh, bias=cols[:, 3:4]).then_inc(h_done, 1)

            def head_body(h, par, first, last):
                for half in range(HALVES):
                    group_turn(h, par, half, first, last, 0, "open")
                    group_turn(h, par, half, first, last, 1, "second")
                    if last and half == 1:
                        for i in range(2, TURNS - 1):
                            half_0_step(i)
                            group_turn(h, par, half, first, last, i, "loop")
                    else:
                        for a, b, chunk in loop_pieces(last, half):
                            with act.Fori(a, b) as i:
                                group_turn(h, par, half, first, last, i, "loop", chunk)
                    if last and half == 1:
                        half_0_step(TURNS - 1)
                    group_turn(h, par, half, first, last, TURNS - 1, "last")

            minus_max_rows(0, 0, 0)
            v_high(TILES - 1, 2 * TURNS - 2, 2, LAST)
            over_heads(act, head_body)
            take_sums(HEADS * HALVES, HEADS * HALVES * TILES)
            act.wait_ge(gate_step, 5)
            heads_high(BASE_TAIL + 2)
            gate(0, 0, mxb[0][:, :])
            gate(0, 1, mxb[1][:, :])
            gate(0, 2, sc[0][:, :])
            act.wait_ge(pv_done, HEADS * HALVES * TILES)
            normalised(1, sc[2])
            hidden(0, mxb[1][:, :])
            gate(1, 0, acc[:, 0, :])
            gate(1, 1, acc[:, 1, :])
            gate(1, 2, mxb[0][:, :])
            hidden(1, sc[1][:, :])

        @block.vector
        def _(dve):
            def layer_norm_mean(src, n0, n1, sem_, v):
                mean = stat[:, 0, n0:n1]
                dve.tensor_reduce(mean, src[:, n0:n1, :], AX.X, ALU.add).then_inc(sem_, 1)
                dve.wait_ge(sem_, v + 1)
                dve.tensor_scalar(mean, mean, 1.0 / DM, None, ALU.mult).then_inc(sem_, 1)

            def layer_norm_centre(src, dst, n0, n1, sem_, v):
                dve.wait_ge(sem_, v + 2)
                mean = stat[:, 0, n0:n1].rearrange("p (n a) -> p n a", a=1).broadcast_to([P, n1 - n0, DM])
                dve.tensor_tensor(dst[:, n0:n1, :], src[:, n0:n1, :], mean, ALU.subtract).then_inc(sem_, 1)

            def layer_norm_square(dst, sq, n0, n1, sem_, v):
                dve.wait_ge(sem_, v + 3)
                dve.tensor_tensor(sq, dst[:, n0:n1, :], dst[:, n0:n1, :], ALU.mult).then_inc(sem_, 1)

            def layer_norm_var(sq, n0, n1, sem_, v):
                dve.wait_ge(sem_, v + 4)
                dve.tensor_reduce(stat[:, 1, n0:n1], sq, AX.X, ALU.add).then_inc(sem_, 1)
                dve.wait_ge(sem_, v + 5)
                dve.tensor_scalar(stat[:, 2, n0:n1], stat[:, 1, n0:n1], 1.0 / DM, EPS, ALU.mult,
                                  ALU.add).then_inc(sem_, 1)

            def layer_norm(src, dst, sq, n0, n1, sem_, v):
                layer_norm_mean(src, n0, n1, sem_, v)
                layer_norm_centre(src, dst, n0, n1, sem_, v)
                layer_norm_square(dst, sq, n0, n1, sem_, v)
                layer_norm_var(sq, n0, n1, sem_, v)

            def layer_norm_end(dst, n0, n1, sem_, v):
                n = n1 - n0
                var = stat[:, 1, n0:n1]
                dve.wait_ge(sem_, v + 6)
                dve.wait_ge(sem_, v + 7)
                dve.tensor_tensor(dst[:, n0:n1, :], dst[:, n0:n1, :],
                                  var.rearrange("p (n a) -> p n a", a=1).broadcast_to([P, n, DM]),
                                  ALU.mult).then_inc(sem_, 1)

            dve.memset(q_low[DH:P, :], 0.0).then_inc(zeros_ready, 1)
            dve.memset(WkT[DH:P, :], 0.0).then_inc(zeros_ready, 1)
            dve.memset(V4[:, WHOLE, :, :], 0.0).then_inc(ones_ready, 1)
            dve.wait_ge(ones_ready, 1)
            dve.memset(V4[0:LAST, WHOLE, :, DH], 1.0).then_inc(ones_ready, 1)

            def q_low_dve(par, half, nh):
                dve.wait_ge(bank_hi, nh)
                dve.tensor_tensor(q_low[0:DH, :], bank[0:DH, :], qA[0:DH, par, half * QG:(half + 1) * QG],
                                  ALU.subtract).then_inc(bank_free, 1)

            def k_low(par, i, nh):
                dve.wait_ge(bank_hi, nh)
                k = K[DH:P, ds(par * KEYS + i * CHUNK, CHUNK)]
                dve.tensor_tensor(k, bank[DH:P, 0:CHUNK], k, ALU.subtract).then_inc(bank_free, 1)

            def x_low(n):
                dve.wait_ge(xT_hi, n + 1)
                s = slice(n * QG, (n + 1) * QG)
                dve.tensor_tensor(xnT_lo[:, s], acc[:, 0, :], xnT_hi[:, s], ALU.subtract).then_inc(xT_lo, 1)

            def context_low(g):
                a, b = g * CT * P, min((g + 1) * CT, TILES) * P
                bank_g = mxb[1][:, :] if g % 2 == 0 else acc[:, 1, :]
                dve.wait_ge(cT_lo_ready, g + 1)
                dve.tensor_copy(ctx_lo[0:DC, a:b], bank_g.bitcast(BF16)[0:DC, 0:b - a]).then_inc(cT_lo, 1)

            dve.wait_ge(load_x[0], 16)
            layer_norm(x_raw, x_raw, x_sq[:, 0:QT, :], 0, QT, ln_step, 0)
            dve.wait_ge(load_x[1], 16)
            layer_norm(x_raw, x_raw, x_sq[:, QT:2 * QT, :], QT, 2 * QT, ln_step2, 0)
            layer_norm_end(x_raw, 0, QT, ln_step, 0)
            for n, (w, hi, lo) in enumerate(((Wk_raw, WkD_hi, WkD_lo), (Wq_raw, WqD_hi, WqD_lo))):
                m = w.shape[0]
                dve.wait_ge(w_hi, n + 1)
                dve.tensor_tensor(lo[0:m, :, :, :], w.rearrange("p (h a d) -> p h a d", h=HEADS, a=1)
                                  .broadcast_to([m, HEADS, 2, DH]), hi[0:m, :, :, :],
                                  ALU.subtract).then_inc(wsplit, 1)
            context_low(0)
            x_low(0)
            context_low(1)
            q_low_dve(0, 0, 1)
            context_low(2)
            k_low(0, 0, 2)
            context_low(3)
            layer_norm_end(x_raw, QT, 2 * QT, ln_step2, 0)
            context_low(4)
            dve.wait_ge(load_bias, 32)
            dve.wait_ge(y_start, 1)
            dve.tensor_scalar(yT[:, :], yT[:, :], cols[:, 4:5], None, ALU.add).then_inc(y_start, 1)
            x_low(1)
            dve.wait_ge(wT_kept, 3)
            dve.tensor_tensor(gateT_lo[:, :, :].rearrange("p a b -> p (a b)"), sc[0][:, :],
                              gateT_hi[:, :, :].rearrange("p a b -> p (a b)"), ALU.subtract).then_inc(gates_split, 1)
            for g in range(5, GROUPS):
                context_low(g)
            k_low(0, 1, 3)
            dve.wait_ge(load_g, 13 * 16)
            for w in range(3):
                dve.tensor_tensor(gsum[:, w, :], gate_raw[:, 3 + w, :], cbc, ALU.mult).then_inc(gate_step, 1)
            dve.wait_ge(gate_step, 3)
            dve.tensor_reduce(gate_bias[:, :], gsum, AX.X, ALU.add).then_inc(gate_step, 1)
            dve.wait_ge(gate_step, 4)
            dve.tensor_tensor(gate_bias[:, :], gate_bias[:, :], cols[:, 0:3], ALU.add).then_inc(gate_step, 1)
            def hand(uses, what):
                n = 0
                for k in uses:
                    if k[0] in ("QP", "K", "OT"):
                        n += 1
                    if k == what:
                        return n
                return n

            hb0 = 2 + TURNS
            hb1 = hb0 + hand(head_uses(True, False), None)
            per = hand(head_uses(False, False), None)
            hbl = hb1 + (HEADS - 2) * per
            hbt = hbl + hand(head_uses(False, True), None)

            def hands(h, first, last, half, what):
                b = hb0 if first else hbl if last else (h - 1) * per + hb1
                if half == 1:
                    b = b + hand(bank_uses(first, last, 0), None)
                return b + hand(bank_uses(first, last, half), what)

            def reduce_max(i, qt, m, fresh):
                if fresh is not None:
                    dve.wait_ge(max_step, fresh)
                dve.wait_ge(mx_ready, m + 1)
                dve.tensor_reduce(part_max[:, qt, ds(i, 1)], mxb[qt % 2][:, 0:MAX_KEYS], AX.X,
                                  ALU.max).then_inc(mx_taken, 1)

            def minus_max(g1):
                dve.wait_ge(mx_taken, g1 * MX)
                if not (isinstance(g1, int) and g1 == 1):
                    dve.wait_ge(max_step, (g1 - 1) * 3)
                dve.tensor_reduce(neg_max[:, :], part_max[:, :, :], AX.X, ALU.max, negate=True).then_inc(max_step, 1)
                dve.wait_ge(max_step, (g1 - 1) * 3 + 1)
                dve.tensor_copy(neg_max2[:, :, 0], neg_max[:, :]).then_inc(max_step, 1)
                dve.wait_ge(max_step, (g1 - 1) * 3 + 2)
                dve.tensor_tensor(neg_max2[:, :, 1], neg_max[:, :], neg_max2[:, :, 0],
                                  ALU.subtract).then_inc(max_step, 1)

            def v_low(t, b, rows):
                dve.wait_ge(v_hi, t + 1)
                v = V[0:rows, ds(t * HEADS * VW, HEADS * VW)].rearrange("p (h c) -> p h c", h=HEADS)
                dve.tensor_tensor(v[:, :, DH + 1:VW], sc[b][0:rows, :].rearrange("p (h c) -> p h c", h=HEADS),
                                  v[:, :, 0:DH], ALU.subtract).then_inc(v_lo_dve, 1)

            def v_turn(i, first, last):
                if not first:
                    reduce_max(i - 1, QT - 1, i * QT - 1, None)
                reduce_max(i, 0, i * QT, None)
                v_low(i * UNROLL, 0, P)
                reduce_max(i, 1, i * QT + 1, None)
                if not last:
                    k_low(0, i + 2, i + 4)
                reduce_max(i, 2, i * QT + 2, None)

            v_turn(0, True, False)
            with dve.Fori(1, TURNS - 2) as i:
                v_turn(i, False, False)
            v_turn(TURNS - 2, False, True)
            reduce_max(TURNS - 2, QT - 1, MX - 1, None)
            minus_max(1)
            v_low(TILES - UNROLL, 0, P)
            q_low_dve(0, 1, TURNS + 2)

            def low_part(n, j, cols=POOL_COLS):
                dve.wait_ge(p_ready, n + 1)
                hi = prob[:, j, :].bitcast(BF16).rearrange("p (q two) -> p q two", two=2)[:, :, 1]
                dve.tensor_tensor(prob_lo[:, j, cols:QG], prob[:, j, cols:QG], hi[:, cols:QG],
                                  ALU.subtract).then_inc(lo_dve, 1)

            def add_output(half, n):
                dve.wait_ge(bank_ready, n + 1)
                y = yT[:, half * QG:(half + 1) * QG]
                dve.tensor_tensor(y, bank[:, :], y, ALU.add).then_inc(bank_free, 1)

            def divide(g1):
                dve.wait_ge(acc_taken, g1)
                dve.reciprocal(rden[:, :], acc_raw[:, :, DH]).then_inc(fin_step, 1)
                dve.tensor_tensor(o_norm[:, :, :], acc_raw[:, :, 0:DH], acc_raw[:, :, DH + 1:VW],
                                  ALU.add).then_inc(fin_step, 1)
                dve.wait_ge(fin_step, (g1 - 1) * 3 + 2)
                dve.tensor_tensor(o_norm[:, :, :], o_norm[:, :, :],
                                  rden[:, :].rearrange("p (n a) -> p n a", a=1).broadcast_to([P, QT, DH]),
                                  ALU.mult).then_inc(fin_step, 1)

            def heads_low(nh):
                dve.wait_ge(bank_hi, nh)
                for a in range(2):
                    m = dve.tensor_tensor(oT4[DH:P, :, a, :],
                                          bank[a * DH:(a + 1) * DH, 0:2 * P].rearrange("p (k q) -> p k q", k=2),
                                          oT4[0:DH, :, a, :], ALU.subtract)
                m.then_inc(bank_free, 1)

            def group_turn(h, par, half, first, last, i, kind, chunk=None):
                g = h * HALVES + half
                n0 = g * TILES + i * UNROLL
                start = first and half == 0 and kind == "open"
                cols = POOL_COLS_FINAL if last and half == 1 else POOL_COLS
                with_maxima = kind != "last" and not (last and half == 1)

                def maxima(qt):
                    if with_maxima:
                        reduce_max(i, qt, (g + 1) * MX + i * QT + qt, g * 3 + 1 if kind == "open" else None)

                if not start:
                    low_part(n0 - 1, UNROLL - 1, POOL_COLS if kind == "open" else cols)
                if kind != "open" and not (last and half == 1):
                    reduce_max(i - 1, QT - 1, (g + 1) * MX + (i - 1) * QT + QT - 1, None)
                if kind == "last" and not (last and half == 1):
                    minus_max(g + 2)
                maxima(0)
                low_part(n0, 0, cols)
                if kind == ("second" if last and half == 1 else "last") and not (first and half == 0):
                    divide(g)
                if kind == "open" and not first:
                    heads_low(hands(h, first, last, half, ("OT", half)))
                if kind == "second" and not last:
                    q_low_dve(1 - par, half, hands(h, first, last, half, ("QP", half)))
                if chunk is not None:
                    k_low(1 - par, i + (chunk - 2), hands(h, first, last, half, ("K", chunk)) + (i - 2))
                maxima(1)
                low_part(n0 + 1, 1, cols)
                maxima(2)
                if kind == "open" and not first:
                    add_output(half, use(h, first, last, half, ("Y", half)))

            def head_body(h, par, first, last):
                for half in range(HALVES):
                    group_turn(h, par, half, first, last, 0, "open")
                    group_turn(h, par, half, first, last, 1, "second")
                    if last and half == 1:
                        for i in range(2, TURNS - 1):
                            half_0_step(i)
                            group_turn(h, par, half, first, last, i, "loop")
                    else:
                        for a, b, chunk in loop_pieces(last, half):
                            with dve.Fori(a, b) as i:
                                group_turn(h, par, half, first, last, i, "loop", chunk)
                    if last and half == 1:
                        half_0_step(TURNS - 1)
                    group_turn(h, par, half, first, last, TURNS - 1, "last")

            def residual(half, b):
                n0, n1 = half * QT, (half + 1) * QT
                dve.wait_ge(y_rows, half + 1)
                dve.tensor_tensor(x1[:, n0:n1, :], b[:, :].rearrange("p (n d) -> p n d", d=DM),
                                  x_late[:, n0:n1, :], ALU.add).then_inc(x1_step, 1)
                dve.wait_ge(x1_step, (1 + LN_STEPS) * half + 1)

            def residual_end(half):
                layer_norm_end(xc, half * QT, (half + 1) * QT, x1_step, (1 + LN_STEPS) * half + 1)

            def normalised_low(half, b):
                dve.wait_ge(xn2_kept, 2 * half + 1)
                dve.tensor_tensor(xn2_lo[half], b[:, :], xn2_hi[half], ALU.subtract).then_inc(xn2_kept, 1)

            def cell(half):
                dve.wait_ge(gate_done, 3 * half + 1)
                dve.tensor_scalar(fT[half], fT[half], cols[:, 5:6], None, ALU.mult).then_inc(cell_step, 1)
                dve.wait_ge(gate_done, 3 * half + 3)
                dve.tensor_tensor(iT[half], iT[half], gT[half], ALU.mult).then_inc(cell_step, 1)
                dve.wait_ge(cell_step, 3 * half + 2)
                dve.tensor_tensor(cT[half], fT[half], iT[half], ALU.add).then_inc(cell_step, 1)

            def result(half, b):
                dve.wait_ge(h_rows, half + 1)
                dve.tensor_tensor(res[half], b[:, :].rearrange("p (n d) -> p n d", d=DM),
                                  x1[:, half * QT:(half + 1) * QT, :], ALU.add).then_inc(res_done, 1)

            def half_0_step(turn):
                if turn == OT_LOW_TURN:
                    heads_low(hbt + 1)
                elif turn == Y_ADD_TURN:
                    add_output(0, BASE_TAIL + 1)
                elif turn == SUM_TURN:
                    dve.wait_ge(load_late, 16)
                    residual(0, mxb[0])
                elif turn == MEAN_TURN:
                    layer_norm_mean(x1, 0, QT, x1_step, 1)
                elif turn == CENTRE_TURN:
                    layer_norm_centre(x1, xc, 0, QT, x1_step, 1)
                    layer_norm_square(xc, sq2[0], 0, QT, x1_step, 1)
                elif turn == VAR_TURN:
                    layer_norm_var(sq2[0], 0, QT, x1_step, 1)
                elif turn == NORM_TURN:
                    residual_end(0)
                elif turn == LOW_TURN:
                    normalised_low(0, mxb[1])

            dve.wait_ge(y_start, 2)
            over_heads(dve, head_body)
            n_last = HEADS * HALVES * TILES
            low_part(n_last - 1, (TILES - 1) % UNROLL, POOL_COLS_FINAL)
            divide(HEADS * HALVES)
            heads_low(hbt + 2)
            add_output(1, BASE_TAIL + 3)
            dve.wait_ge(pv_done, n_last)
            residual(1, sc[1])
            layer_norm(x1, xc, sq2[1], QT, 2 * QT, x1_step, LN_STEPS + 2)
            cell(0)
            residual_end(1)
            normalised_low(1, sc[2])
            cell(1)
            result(0, sc[0])
            result(1, sc[2])


_INS = ["x", "ctx_768", "L0_xattn_Wq", "L0_xattn_Wk", "L0_xattn_Wv", "L0_xattn_Wo", "L0_xattn_bo",
        "L0_ffn_wf", "L0_ffn_uf", "L0_ffn_bf", "L0_ffn_wi", "L0_ffn_ui", "L0_ffn_bi",
        "L0_ffn_wc", "L0_ffn_uc", "L0_ffn_bc", "L0_ffn_wo", "L0_ffn_uo", "L0_ffn_bo", "L0_ffn_in_c"]


def kernel(**inputs):
    import numpy as _np
    import concourse.bacc as _bacc
    from concourse import mybir as _mybir
    from concourse.bass_utils import run_bass_kernel_spmd as _run

    nc = _bacc.Bacc("TRN2", target_bir_lowering=False, num_devices=1)
    arrays, args = {}, []
    for name in _INS:
        a = _np.ascontiguousarray(inputs[name])
        arrays[f"in_{name}_dram"] = a
        args.append(nc.dram_tensor(f"in_{name}_dram", a.shape, _mybir.dt.from_np(a.dtype), kind="ExternalInput").ap())
    out = nc.dram_tensor("out_0_dram", (1, NQ, DM), _mybir.dt.float32, kind="ExternalOutput").ap()
    build(nc, *args, out)
    r = _run(nc, [arrays], core_ids=[0])
    return r.results[0]["out_0_dram"]
```
